# Optimizing a Trainium2 kernel written in Bass

```python
import numpy as np
import jax
import jax.numpy as jnp

def _softmax(x, axis=-1):
    return jax.nn.softmax(x, axis=axis)

def _gelu(x):
    return jax.nn.gelu(x, approximate=True)

def _silu(x):
    return jax.nn.silu(x)

def _sigmoid(x):
    return jax.nn.sigmoid(x)

def _layernorm(x, axis=-1, eps=1e-05):
    m = jnp.mean(x, axis=axis, keepdims=True)
    v = jnp.var(x, axis=axis, keepdims=True)
    return (x - m) / jnp.sqrt(v + eps)

def _scatter_add(tgt, idx, src, axis=0):
    return tgt.at[idx].add(src)

def _segment_sum(src, seg, n):
    return jax.ops.segment_sum(src, seg, n)
kernel_name = 'mk_dlrm_tower_d1_rec_r8_d66786'

def setup_inputs(seed: int=0):
    np.random.seed(seed)
    _w = jnp.asarray

    def _rec_inputs():
        import jax
        import jax.numpy as jnp
        _tk = jax.random.key(seed)
        dense_ctx = jax.random.normal(jax.random.fold_in(_tk, 190), (1024, 16), jnp.float32)
        ids = jnp.stack([jax.random.randint(jax.random.fold_in(_tk, 200 + f), (1024,), 0, v, jnp.int32) for f, v in enumerate([125000, 125000, 12500, 1000, 1250, 12500, 12500, 12500, 1000, 125000, 125000, 12500, 1000, 1250, 1000, 12500, 1250, 12500, 125000, 1000, 1000, 125000, 1250, 1000, 1000, 125000, 1000, 12500, 1000, 1000, 125000, 1000, 1000, 12500, 12500, 12500, 1250, 12500, 1000])], axis=1)
        tbl_0 = 0.05 * jax.random.normal(jax.random.fold_in(_tk, 500 + 0), (125000, 16), jnp.float32)
        tbl_1 = 0.05 * jax.random.normal(jax.random.fold_in(_tk, 500 + 1), (125000, 16), jnp.float32)
        tbl_2 = 0.05 * jax.random.normal(jax.random.fold_in(_tk, 500 + 2), (12500, 16), jnp.float32)
        tbl_3 = 0.05 * jax.random.normal(jax.random.fold_in(_tk, 500 + 3), (1000, 16), jnp.float32)
        tbl_4 = 0.05 * jax.random.normal(jax.random.fold_in(_tk, 500 + 4), (1250, 16), jnp.float32)
        tbl_5 = 0.05 * jax.random.normal(jax.random.fold_in(_tk, 500 + 5), (12500, 16), jnp.float32)
        tbl_6 = 0.05 * jax.random.normal(jax.random.fold_in(_tk, 500 + 6), (12500, 16), jnp.float32)
        tbl_7 = 0.05 * jax.random.normal(jax.random.fold_in(_tk, 500 + 7), (12500, 16), jnp.float32)
        tbl_8 = 0.05 * jax.random.normal(jax.random.fold_in(_tk, 500 + 8), (1000, 16), jnp.float32)
        tbl_9 = 0.05 * jax.random.normal(jax.random.fold_in(_tk, 500 + 9), (125000, 16), jnp.float32)
        tbl_10 = 0.05 * jax.random.normal(jax.random.fold_in(_tk, 500 + 10), (125000, 16), jnp.float32)
        tbl_11 = 0.05 * jax.random.normal(jax.random.fold_in(_tk, 500 + 11), (12500, 16), jnp.float32)
        tbl_12 = 0.05 * jax.random.normal(jax.random.fold_in(_tk, 500 + 12), (1000, 16), jnp.float32)
        tbl_13 = 0.05 * jax.random.normal(jax.random.fold_in(_tk, 500 + 13), (1250, 16), jnp.float32)
        tbl_14 = 0.05 * jax.random.normal(jax.random.fold_in(_tk, 500 + 14), (1000, 16), jnp.float32)
        tbl_15 = 0.05 * jax.random.normal(jax.random.fold_in(_tk, 500 + 15), (12500, 16), jnp.float32)
        tbl_16 = 0.05 * jax.random.normal(jax.random.fold_in(_tk, 500 + 16), (1250, 16), jnp.float32)
        tbl_17 = 0.05 * jax.random.normal(jax.random.fold_in(_tk, 500 + 17), (12500, 16), jnp.float32)
        tbl_18 = 0.05 * jax.random.normal(jax.random.fold_in(_tk, 500 + 18), (125000, 16), jnp.float32)
        tbl_19 = 0.05 * jax.random.normal(jax.random.fold_in(_tk, 500 + 19), (1000, 16), jnp.float32)
        tbl_20 = 0.05 * jax.random.normal(jax.random.fold_in(_tk, 500 + 20), (1000, 16), jnp.float32)
        tbl_21 = 0.05 * jax.random.normal(jax.random.fold_in(_tk, 500 + 21), (125000, 16), jnp.float32)
        tbl_22 = 0.05 * jax.random.normal(jax.random.fold_in(_tk, 500 + 22), (1250, 16), jnp.float32)
        tbl_23 = 0.05 * jax.random.normal(jax.random.fold_in(_tk, 500 + 23), (1000, 16), jnp.float32)
        tbl_24 = 0.05 * jax.random.normal(jax.random.fold_in(_tk, 500 + 24), (1000, 16), jnp.float32)
        tbl_25 = 0.05 * jax.random.normal(jax.random.fold_in(_tk, 500 + 25), (125000, 16), jnp.float32)
        tbl_26 = 0.05 * jax.random.normal(jax.random.fold_in(_tk, 500 + 26), (1000, 16), jnp.float32)
        tbl_27 = 0.05 * jax.random.normal(jax.random.fold_in(_tk, 500 + 27), (12500, 16), jnp.float32)
        tbl_28 = 0.05 * jax.random.normal(jax.random.fold_in(_tk, 500 + 28), (1000, 16), jnp.float32)
        tbl_29 = 0.05 * jax.random.normal(jax.random.fold_in(_tk, 500 + 29), (1000, 16), jnp.float32)
        tbl_30 = 0.05 * jax.random.normal(jax.random.fold_in(_tk, 500 + 30), (125000, 16), jnp.float32)
        tbl_31 = 0.05 * jax.random.normal(jax.random.fold_in(_tk, 500 + 31), (1000, 16), jnp.float32)
        tbl_32 = 0.05 * jax.random.normal(jax.random.fold_in(_tk, 500 + 32), (1000, 16), jnp.float32)
        tbl_33 = 0.05 * jax.random.normal(jax.random.fold_in(_tk, 500 + 33), (12500, 16), jnp.float32)
        tbl_34 = 0.05 * jax.random.normal(jax.random.fold_in(_tk, 500 + 34), (12500, 16), jnp.float32)
        tbl_35 = 0.05 * jax.random.normal(jax.random.fold_in(_tk, 500 + 35), (12500, 16), jnp.float32)
        tbl_36 = 0.05 * jax.random.normal(jax.random.fold_in(_tk, 500 + 36), (1250, 16), jnp.float32)
        tbl_37 = 0.05 * jax.random.normal(jax.random.fold_in(_tk, 500 + 37), (12500, 16), jnp.float32)
        tbl_38 = 0.05 * jax.random.normal(jax.random.fold_in(_tk, 500 + 38), (1000, 16), jnp.float32)
        _rk = jax.random.fold_in(_tk, 7)
        W_top1 = 0.0606339 * jax.random.normal(jax.random.fold_in(_tk, 801), (272, 512), jnp.float32)
        W_top2 = 0.0441942 * jax.random.normal(jax.random.fold_in(_tk, 802), (512, 256), jnp.float32)
        W_top3 = 0.0625 * jax.random.normal(jax.random.fold_in(_tk, 803), (256, 1), jnp.float32)
        b_top1 = jnp.zeros((512,), jnp.float32)
        b_top2 = jnp.zeros((256,), jnp.float32)
        return (dense_ctx, ids, tbl_0, tbl_1, tbl_2, tbl_3, tbl_4, tbl_5, tbl_6, tbl_7, tbl_8, tbl_9, tbl_10, tbl_11, tbl_12, tbl_13, tbl_14, tbl_15, tbl_16, tbl_17, tbl_18, tbl_19, tbl_20, tbl_21, tbl_22, tbl_23, tbl_24, tbl_25, tbl_26, tbl_27, tbl_28, tbl_29, tbl_30, tbl_31, tbl_32, tbl_33, tbl_34, tbl_35, tbl_36, tbl_37, tbl_38, W_top1, b_top1, W_top2, b_top2, W_top3)
    dense_ctx, ids, tbl_0, tbl_1, tbl_2, tbl_3, tbl_4, tbl_5, tbl_6, tbl_7, tbl_8, tbl_9, tbl_10, tbl_11, tbl_12, tbl_13, tbl_14, tbl_15, tbl_16, tbl_17, tbl_18, tbl_19, tbl_20, tbl_21, tbl_22, tbl_23, tbl_24, tbl_25, tbl_26, tbl_27, tbl_28, tbl_29, tbl_30, tbl_31, tbl_32, tbl_33, tbl_34, tbl_35, tbl_36, tbl_37, tbl_38, W_top1, b_top1, W_top2, b_top2, W_top3 = _rec_inputs()

    def _L0_rec_setup():
        import jax, jax.numpy as jnp
        import numpy as np
        B, F, D = (1024, 39, 16)
        HIDDEN = [128, 128, 128]

        def _cin(x, Ws, bs):
            F0 = x.shape[1]
            h = x
            outs = []
            n = len(Ws)
            for i, (W, b) in enumerate(zip(Ws, bs)):
                L = W.shape[-1]
                Fk = h.shape[1]
                Wr = W.reshape(F0, Fk, L)
                z = jnp.einsum('bfd,bgd->bfgd', x, h)
                cur = jax.nn.relu(jnp.einsum('bfgd,fgl->bld', z, Wr) + b[None, :, None])
                if i != n - 1:
                    h = cur[:, :L // 2]
                    direct = cur[:, L // 2:]
                else:
                    direct = cur
                outs.append(direct)
            return jnp.concatenate(outs, axis=1).sum(-1)
        key = jax.random.key(seed)
        ks = jax.random.split(key, 8)
        x = jax.random.normal(ks[0], (B, F, D), dtype=jnp.float32)
        field_nums = [F]
        Ws, bs = ([], [])
        for i, L in enumerate(HIDDEN):
            fan_in = field_nums[0] * field_nums[-1]
            lim = np.sqrt(6.0 / fan_in)
            Ws.append(jax.random.uniform(ks[1 + i], (fan_in, L), jnp.float32, -lim, lim))
            bs.append(jnp.zeros((L,), jnp.float32))
            field_nums.append(L // 2)
        return {'x': x, 'W0': Ws[0], 'W1': Ws[1], 'W2': Ws[2], 'b0': bs[0], 'b1': bs[1], 'b2': bs[2]}
    _L0_rec_all = _L0_rec_setup()
    _L0_rec_in = {k: v for k, v in _L0_rec_all.items() if k in ('W0', 'W1', 'W2', 'b0', 'b1', 'b2')}
    del _L0_rec_all
    return {'dense_ctx': dense_ctx, 'ids': ids, 'tbl_0': tbl_0, 'tbl_1': tbl_1, 'tbl_2': tbl_2, 'tbl_3': tbl_3, 'tbl_4': tbl_4, 'tbl_5': tbl_5, 'tbl_6': tbl_6, 'tbl_7': tbl_7, 'tbl_8': tbl_8, 'tbl_9': tbl_9, 'tbl_10': tbl_10, 'tbl_11': tbl_11, 'tbl_12': tbl_12, 'tbl_13': tbl_13, 'tbl_14': tbl_14, 'tbl_15': tbl_15, 'tbl_16': tbl_16, 'tbl_17': tbl_17, 'tbl_18': tbl_18, 'tbl_19': tbl_19, 'tbl_20': tbl_20, 'tbl_21': tbl_21, 'tbl_22': tbl_22, 'tbl_23': tbl_23, 'tbl_24': tbl_24, 'tbl_25': tbl_25, 'tbl_26': tbl_26, 'tbl_27': tbl_27, 'tbl_28': tbl_28, 'tbl_29': tbl_29, 'tbl_30': tbl_30, 'tbl_31': tbl_31, 'tbl_32': tbl_32, 'tbl_33': tbl_33, 'tbl_34': tbl_34, 'tbl_35': tbl_35, 'tbl_36': tbl_36, 'tbl_37': tbl_37, 'tbl_38': tbl_38, 'W_top1': W_top1, 'b_top1': b_top1, 'W_top2': W_top2, 'b_top2': b_top2, 'W_top3': W_top3, 'L0_rec_W0': _L0_rec_in['W0'], 'L0_rec_W1': _L0_rec_in['W1'], 'L0_rec_W2': _L0_rec_in['W2'], 'L0_rec_b0': _L0_rec_in['b0'], 'L0_rec_b1': _L0_rec_in['b1'], 'L0_rec_b2': _L0_rec_in['b2']}

def reference(dense_ctx, ids, tbl_0, tbl_1, tbl_2, tbl_3, tbl_4, tbl_5, tbl_6, tbl_7, tbl_8, tbl_9, tbl_10, tbl_11, tbl_12, tbl_13, tbl_14, tbl_15, tbl_16, tbl_17, tbl_18, tbl_19, tbl_20, tbl_21, tbl_22, tbl_23, tbl_24, tbl_25, tbl_26, tbl_27, tbl_28, tbl_29, tbl_30, tbl_31, tbl_32, tbl_33, tbl_34, tbl_35, tbl_36, tbl_37, tbl_38, W_top1, b_top1, W_top2, b_top2, W_top3, L0_rec_W0, L0_rec_W1, L0_rec_W2, L0_rec_b0, L0_rec_b1, L0_rec_b2):
    import jax
    import jax.numpy as jnp

    def _L0_rec_ref(x, W0, W1, W2, b0, b1, b2):
        import jax, jax.numpy as jnp
        import numpy as np
        B, F, D = (1024, 39, 16)
        HIDDEN = [128, 128, 128]

        def _cin(x, Ws, bs):
            F0 = x.shape[1]
            h = x
            outs = []
            n = len(Ws)
            for i, (W, b) in enumerate(zip(Ws, bs)):
                L = W.shape[-1]
                Fk = h.shape[1]
                Wr = W.reshape(F0, Fk, L)
                z = jnp.einsum('bfd,bgd->bfgd', x, h)
                cur = jax.nn.relu(jnp.einsum('bfgd,fgl->bld', z, Wr) + b[None, :, None])
                if i != n - 1:
                    h = cur[:, :L // 2]
                    direct = cur[:, L // 2:]
                else:
                    direct = cur
                outs.append(direct)
            return jnp.concatenate(outs, axis=1).sum(-1)
        return _cin(x, [W0, W1, W2], [b0, b1, b2])
    e = jnp.stack([tbl_0[ids[:, 0]], tbl_1[ids[:, 1]], tbl_2[ids[:, 2]], tbl_3[ids[:, 3]], tbl_4[ids[:, 4]], tbl_5[ids[:, 5]], tbl_6[ids[:, 6]], tbl_7[ids[:, 7]], tbl_8[ids[:, 8]], tbl_9[ids[:, 9]], tbl_10[ids[:, 10]], tbl_11[ids[:, 11]], tbl_12[ids[:, 12]], tbl_13[ids[:, 13]], tbl_14[ids[:, 14]], tbl_15[ids[:, 15]], tbl_16[ids[:, 16]], tbl_17[ids[:, 17]], tbl_18[ids[:, 18]], tbl_19[ids[:, 19]], tbl_20[ids[:, 20]], tbl_21[ids[:, 21]], tbl_22[ids[:, 22]], tbl_23[ids[:, 23]], tbl_24[ids[:, 24]], tbl_25[ids[:, 25]], tbl_26[ids[:, 26]], tbl_27[ids[:, 27]], tbl_28[ids[:, 28]], tbl_29[ids[:, 29]], tbl_30[ids[:, 30]], tbl_31[ids[:, 31]], tbl_32[ids[:, 32]], tbl_33[ids[:, 33]], tbl_34[ids[:, 34]], tbl_35[ids[:, 35]], tbl_36[ids[:, 36]], tbl_37[ids[:, 37]], tbl_38[ids[:, 38]]], axis=1)
    z = _L0_rec_ref(e, L0_rec_W0, L0_rec_W1, L0_rec_W2, L0_rec_b0, L0_rec_b1, L0_rec_b2)
    z = z.reshape(z.shape[0], -1)
    h = jnp.concatenate([z, dense_ctx], axis=1)
    h = jnp.maximum(h @ W_top1 + b_top1, 0.0)
    h = jnp.maximum(h @ W_top2 + b_top2, 0.0)
    y = h @ W_top3
    return y

_drawn_inputs = setup_inputs


def setup_inputs(seed=0):
    import zlib

    import numpy as np

    out = dict(_drawn_inputs(seed))
    spreads = {'b_top1': (0.0, 2.0),
     'b_top2': (0.0, 2.0),
     'L0_rec_b0': (0.0, 0.325),
     'L0_rec_b1': (0.0, 0.48),
     'L0_rec_b2': (0.0, 0.8)}
    factors = {'tbl_0': 8.0,
     'tbl_1': 8.0,
     'tbl_2': 8.0,
     'tbl_3': 8.0,
     'tbl_4': 8.0,
     'tbl_5': 8.0,
     'tbl_6': 8.0,
     'tbl_7': 8.0,
     'tbl_8': 8.0,
     'tbl_9': 8.0,
     'tbl_10': 8.0,
     'tbl_11': 8.0,
     'tbl_12': 8.0,
     'tbl_13': 8.0,
     'tbl_14': 8.0,
     'tbl_15': 8.0,
     'tbl_16': 8.0,
     'tbl_17': 8.0,
     'tbl_18': 8.0,
     'tbl_19': 8.0,
     'tbl_20': 8.0,
     'tbl_21': 8.0,
     'tbl_22': 8.0,
     'tbl_23': 8.0,
     'tbl_24': 8.0,
     'tbl_25': 8.0,
     'tbl_26': 8.0,
     'tbl_27': 8.0,
     'tbl_28': 8.0,
     'tbl_29': 8.0,
     'tbl_30': 8.0,
     'tbl_31': 8.0,
     'tbl_32': 8.0,
     'tbl_33': 8.0,
     'tbl_34': 8.0,
     'tbl_35': 8.0,
     'tbl_36': 8.0,
     'tbl_37': 8.0,
     'tbl_38': 8.0,
     'L0_rec_W0': 8.0,
     'L0_rec_W1': 5.692,
     'L0_rec_W2': 4.728,
     'dense_ctx': 8.0}
    for name, (base, spread) in spreads.items():
        noise = np.random.default_rng([zlib.crc32(name.encode()), seed]).standard_normal(out[name].shape)
        drawn = base * np.exp(spread * noise) if base else spread * noise
        out[name] = jnp.asarray(drawn.astype(out[name].dtype))
    for name, factor in factors.items():
        out[name] = (out[name] * factor).astype(out[name].dtype)
    return out
```

```python
from contextlib import ExitStack

import numpy as np
import concourse.bass as bass
from concourse import mybir

FP32 = mybir.dt.float32
BF16 = mybir.dt.bfloat16
ALU = mybir.AluOpType
ACT = mybir.ActivationFunctionType

B, F, D = 1024, 39, 16
L, H = 128, 64
BT = 128
NBT = B // BT
N = 512
DQ = N // BT
CPB = D // DQ
NCHUNK = NBT * CPB

SHIFTS = F // 2 + 1
SPT = 128 // F
R0 = SPT * F
T0 = -(-SHIFTS // SPT)
R0_LAST = (SHIFTS - (T0 - 1) * SPT) * F
T1 = -(-F // 2)
XPAIRS = T1 // 2
G0 = T0 // 2 + 1
GROUPS = 2 * XPAIRS + G0
SELS = G0 + XPAIRS
ZSLOTS = 8
PIECES = 3
KS = PIECES * F
COPIES = 1 + XPAIRS

K_TOP = 272
M_TOP1 = 512
M_TOP2 = 256
DENSE = 16
COL_H0, COL_D0, COL_H1, COL_D1, COL_B2 = range(5)
COL_BT1 = 5
COL_BT2 = COL_BT1 + M_TOP1 // 128
COL_W3 = COL_BT2 + M_TOP2 // 128
COLS = COL_W3 + M_TOP2 // 128
ADDS = CPB - 1
N_CONST = 12


def layer0_tiles(g):
    return [T0 - 1] if g == 0 else [2 * g - 2, 2 * g - 1]


def build(nc, dense_t, ids, tables, w0_fwd, w0_rev, w1, w2,
          wt1, wt2, columns, sel0, selx, ident, out):
    with ExitStack() as ctx:
        def sb(name, shape, dt=FP32):
            return ctx.enter_context(nc.sbuf_tensor(name, shape, dt))

        def psum(name, shape, dt=FP32):
            return ctx.enter_context(nc.psum_tensor(name, shape, dt))

        def sem(name):
            return ctx.enter_context(nc.semaphore(name))

        idx = sb("idx", [BT, F], mybir.dt.int32)
        emb = sb("emb", [BT, F * D])
        rest = sb("rest", [BT, F * D])
        pieces = sb("pieces", [BT, PIECES, F * D], BF16)
        xs = sb("xs", [KS, D * BT], BF16)
        w0_sb = sb("w0_sb", [R0, T0, L])
        w0r_sb = sb("w0r_sb", [R0, T0, L])
        w1_sb = sb("w1_sb", [128, T1, L])
        w2_sb = sb("w2_sb", [128, T1, L])
        sel0_sb = sb("sel0_sb", [KS, T0 + 1, R0], BF16)
        selx_sb = sb("selx_sb", [KS, T1, 128], BF16)
        ident_sb = sb("ident_sb", [128, 128], BF16)
        cols_sb = sb("cols_sb", [128, COLS])
        wt1_sb = sb("wt1_sb", [128, 2, M_TOP1])
        wt1d_sb = sb("wt1d_sb", [DENSE, M_TOP1])
        wt2_sb = sb("wt2_sb", [128, M_TOP1 // 128, M_TOP2])
        dense_sb = sb("dense_sb", [DENSE, B])
        xdup = sb("xdup", [R0, N])
        xb = sb("xb", [128, T1, N])
        h1 = sb("h1", [128, N])
        h2 = sb("h2", [128, N])
        z = sb("z", [128, ZSLOTS, 2, N])
        dir01 = sb("dir01", [128, 2, N])
        dir2 = sb("dir2", [128, 2, N])
        sum01 = sb("sum01", [128, N])
        sum2 = sb("sum2", [128, N])
        half = sb("half", [128, 2, N // 2])
        feat = sb("feat", [128, 2, B])
        t1 = z[:, 0:2, :, :].rearrange("p a b n -> p (a b) n")
        t2 = z[:, 2, :, :]
        y_sb = sb("y_sb", [1, B])

        acc0 = psum("acc0", [128, N])
        acc1 = psum("acc1", [128, N])
        acc2 = psum("acc2", [128, N])
        turned = psum("turned", [128, 2 * N], BF16)
        selp = psum("selp", [128, 2, 2, N])

        const_in = sem("const_in")
        w0_in = sem("w0_in")
        w0_zeroed = sem("w0_zeroed")
        w0_ready = sem("w0_ready")
        idx_in = sem("idx_in")
        gather_turns = sem("gather_turns")
        gathered = sem("gathered")
        split = sem("split")
        turned_ready = sem("turned_ready")
        xs_ready = sem("xs_ready")
        sel_ready = sem("sel_ready")
        sel_copied = sem("sel_copied")
        z_ready = sem("z_ready")
        multiplied = sem("multiplied")
        h_ready = [sem(f"h{i + 1}_ready") for i in range(2)]
        dir_ready = [sem(f"dir{i}_ready") for i in range(3)]
        sum01_done = sem("sum01_done")
        sum2_done = sem("sum2_done")
        folded = sem("folded")
        top_acc = sem("top_acc")
        top_act = sem("top_act")
        y_ready = sem("y_ready")
        y_out = sem("y_out")

        block = ctx.enter_context(nc.Block())

        def zi(s, phase, g, last=False):
            off = {"L1": 0, "L0": XPAIRS, "L2": XPAIRS if last else XPAIRS + G0}[phase]
            return G0 + GROUPS * s + off + g

        def zslot(q, phase, g, last=False):
            return zi(q, phase, g, last) % ZSLOTS

        def wait_past(eng, sem, n):
            if not isinstance(n, int) or n > 0:
                eng.wait_ge(sem, n)

        def steps(eng, body):
            for q in range(CPB):
                body(0, q, False)
            with eng.Fori(1, NBT - 1) as bt:
                for q in range(CPB):
                    body(bt, q, False)
            for q in range(CPB):
                body(NBT - 1, q, q == CPB - 1)

        def dir_freed(bt, q):
            return ADDS * bt + (q - 1 if q < 2 else 1)

        def more(bt):
            return not isinstance(bt, int) or bt < NBT - 1

        @block.sync
        def _(sp):
            def load_idx(bt):
                sp.dma_start(idx[:, :], ids[bass.ds(bt * BT, BT), :]).then_inc(idx_in, 16)

            load_idx(0)
            body = (T0 - 1) * R0
            sp.dma_start(w0_sb[:, 0:T0 - 1, :], w0_fwd[0:body, :].rearrange("(t p) l -> p t l", p=R0)).then_inc(w0_in, 16)
            sp.dma_start(w0_sb[0:R0_LAST, T0 - 1, :], w0_fwd[body:body + R0_LAST, :]).then_inc(w0_in, 16)
            sp.wait_ge(w0_zeroed, 1)
            sp.dma_start(w0r_sb[F:R0, 0, :], w0_rev[F:R0, :]).then_inc(w0_in, 16)
            sp.dma_start(w0r_sb[:, 1:T0 - 1, :], w0_rev[R0:body, :].rearrange("(t p) l -> p t l", p=R0)).then_inc(w0_in, 16)
            sp.dma_start(w0r_sb[0:R0_LAST, T0 - 1, :], w0_rev[body:body + R0_LAST, :]).then_inc(w0_in, 16)

            def prefetch(bt):
                sp.wait_ge(gathered, 16 * F * (bt + 1))
                load_idx(bt + 1)

            with sp.Fori(0, NBT - 1) as bt:
                prefetch(bt)
            sp.wait_ge(y_ready, 2)
            sp.dma_start(out, y_sb[:, :]).then_inc(y_out, 16)
            sp.wait_ge(y_out, 16)

        @block.gpsimd
        def _(pool):
            def gather(bt, f0, f1):
                if f0 == 0:
                    pool.wait_ge(idx_in, 16 * (bt + 1))
                    wait_past(pool, split, 4 * bt)
                    if not isinstance(bt, int):
                        pool.sem_inc(gather_turns)
                for f in range(f0, f1):
                    pool.indirect_dma_start(
                        out=emb[:, f * D:(f + 1) * D], out_offset=None, in_=tables[f],
                        in_offset=bass.IndirectOffsetOnAxis(ap=idx[:, f:f + 1], axis=0),
                    ).then_inc(gathered, 16)

            def add_chunk(total, direct, bt, q, done):
                if q > 1:
                    pool.wait_ge(done, ADDS * bt + q - 1)
                pool.tensor_tensor(total[:, :], direct[:, 0, :] if q == 1 else total[:, :], direct[:, q % 2, :],
                                   ALU.add).then_inc(done, 1)

            def step(bt, q, last):
                s = bt * CPB + q
                if q < 2 and more(bt):
                    gather(bt + 1, *((0, F // 2) if q == 0 else (F // 2, F)))
                if q == 0:
                    return
                if q == 1:
                    wait_past(pool, folded, 4 * bt)
                pool.wait_ge(dir_ready[0], s + 1)
                pool.wait_ge(dir_ready[1], s + 1)
                add_chunk(sum01, dir01, bt, q, sum01_done)
                pool.wait_ge(dir_ready[2], s + 1)
                add_chunk(sum2, dir2, bt, q, sum2_done)
                if q == CPB - 1:
                    for i, (total, done) in enumerate(((sum01, sum01_done), (sum2, sum2_done))):
                        pool.wait_ge(done, ADDS * (bt + 1))
                        pool.tensor_tensor(half[:, i, :], total[:, 0:N // 2], total[:, N // 2:N], ALU.add).then_inc(folded, 1)
                    for i in range(2):
                        pool.wait_ge(folded, 1)
                        pool.wait_ge(folded, 4 * bt + 1 + i)
                        pool.tensor_tensor(feat[:, i, bass.ds(bt * BT, BT)], half[:, i, 0:BT], half[:, i, BT:2 * BT],
                                           ALU.add).then_inc(folded, 1)

            gather(0, 0, F)
            steps(pool, step)

        @block.scalar
        def _(act):
            def load(dst, src):
                act.dma_start(dst, src).then_inc(const_in, 16)

            load(ident_sb[:, :], ident)
            load(sel0_sb[:, :, :], sel0)
            load(selx_sb[:, :, :], selx)
            load(cols_sb[:, :], columns)
            body = (T1 - 1) * 128
            for dst, src in ((w1_sb, w1), (w2_sb, w2)):
                load(dst[:, 0:T1 - 1, :], src[0:body, :].rearrange("(t p) l -> p t l", p=128))
                load(dst[0:H, T1 - 1, :], src[body:body + H, :])
            load(wt1_sb[:, :, :], wt1[0:256, :].rearrange("(c p) m -> p c m", p=128))
            load(wt1d_sb[:, :], wt1[256:K_TOP, :])
            load(wt2_sb[:, :, :], wt2.rearrange("(c p) m -> p c m", p=128))
            load(dense_sb[:, :], dense_t)
            act.wait_ge(const_in, 16 * N_CONST)

            def turn_copy(bt, hf):
                act.wait_ge(turned_ready, 2 * bt + hf + 1)
                act.activation(xs[:, hf * 2 * N:(hf + 1) * 2 * N], turned[0:KS, :], ACT.Copy).then_inc(xs_ready, 1)

            def dup_copy(c):
                act.wait_ge(sel_ready, SELS * c + 1)
                act.activation(xdup[:, :], selp[0:R0, 0, 0, :], ACT.Copy).then_inc(sel_copied, 1)

            def xb_copy(c, j, q, first=False):
                act.wait_ge(sel_ready, SELS * c + G0 + j + 1)
                if not first:
                    act.wait_ge(z_ready, zi(c - 1, "L2", j) + 1)
                act.activation(xb[:, 2 * j:2 * j + 2, :], selp[:, j % 2, :, :], ACT.Copy).then_inc(sel_copied, 1)

            def relu(dst, src, col, rows=slice(0, 128)):
                return act.activation(dst, src, ACT.Relu, bias=cols_sb[rows, col:col + 1])

            def evacuate0(s, nxt, first=False):
                act.wait_ge(multiplied, G0 if first else zi(s, "L0", G0 - 1) + 1)
                for p in (0, H):
                    relu(h1[p:p + H, :], acc0[0:H, :], COL_H0, slice(0, H)).then_inc(h_ready[0], 1)
                wait_past(act, sum01_done, dir_freed(*nxt))
                relu(dir01[0:H, nxt[1] % 2, :], acc0[H:128, :], COL_D0, slice(H, 128)).then_inc(dir_ready[0], 1)

            def evacuate1(s, q):
                act.wait_ge(multiplied, zi(s, "L1", XPAIRS - 1) + 1)
                for p in (0, H):
                    relu(h2[p:p + H, :], acc1[0:H, :], COL_H1, slice(0, H)).then_inc(h_ready[1], 1)
                relu(dir01[H:128, q % 2, :], acc1[H:128, :], COL_D1, slice(H, 128)).then_inc(dir_ready[1], 1)

            def evacuate2(bt, s, q, last):
                act.wait_ge(multiplied, zi(s, "L2", XPAIRS - 1, last) + 1)
                wait_past(act, sum2_done, dir_freed(bt, q))
                relu(dir2[:, q % 2, :], acc2[:, :], COL_B2).then_inc(dir_ready[2], 1)

            turn_copy(0, 0)
            turn_copy(0, 1)
            dup_copy(0)
            for j in range(XPAIRS):
                xb_copy(0, j, 0, first=True)
            evacuate0(-1, (0, 0), first=True)

            def step(bt, q, last):
                s = bt * CPB + q
                if not last:
                    dup_copy(s + 1)
                evacuate1(s, q)
                if not last:
                    evacuate0(s, (bt, q + 1) if q < CPB - 1 else (bt + 1, 0))
                    for j in range(XPAIRS):
                        xb_copy(s + 1, j, q)
                        if j == 6 and q >= 2 and more(bt):
                            turn_copy(bt + 1, q - 2)
                evacuate2(bt, s, q, last)

            steps(act, step)

            na = 0
            for nh in range(B // N):
                for m in range(M_TOP1 // 128):
                    na += 1
                    act.wait_ge(top_acc, na)
                    act.activation(t1[:, m, :], [acc0, acc1, acc2][m % 3][:, :], ACT.Relu,
                                   bias=cols_sb[:, COL_BT1 + m:COL_BT1 + m + 1]).then_inc(top_act, 1)
                for m in range(M_TOP2 // 128):
                    na += 1
                    act.wait_ge(top_acc, na)
                    act.activation(t2[:, m, :], selp[:, 0, m, :], ACT.Relu,
                                   bias=cols_sb[:, COL_BT2 + m:COL_BT2 + m + 1]).then_inc(top_act, 1)
                na += 1
                act.wait_ge(top_acc, na)
                act.activation(y_sb[:, nh * N:(nh + 1) * N], selp[0:1, 1, 0, :], ACT.Copy).then_inc(y_ready, 1)

        @block.vector
        def _(dve):
            dve.memset(w0r_sb[:, 0, :], 0.0).then_inc(w0_zeroed, 1)
            dve.wait_ge(w0_in, 16 * 5)
            dve.wait_ge(w0_zeroed, 1)
            dve.tensor_tensor(w0_sb[:, 0:T0 - 1, :], w0_sb[:, 0:T0 - 1, :], w0r_sb[:, 0:T0 - 1, :], ALU.add).then_inc(w0_ready, 1)
            dve.tensor_tensor(w0_sb[0:R0_LAST, T0 - 1, :], w0_sb[0:R0_LAST, T0 - 1, :], w0r_sb[0:R0_LAST, T0 - 1, :],
                              ALU.add).then_inc(w0_ready, 1)

            def split_step(bt, i, first=False):
                if i == 0:
                    dve.wait_ge(gathered, 16 * F * (bt + 1))
                    if not first:
                        dve.wait_ge(turned_ready, 2 * bt)
                else:
                    dve.wait_ge(split, 4 * bt + i)
                if i == 0:
                    ins = dve.tensor_copy(pieces[:, 0, :], emb[:, :])
                elif i == 1:
                    ins = dve.tensor_tensor(rest[:, :], emb[:, :], pieces[:, 0, :], ALU.subtract)
                elif i == 2:
                    ins = dve.tensor_copy(pieces[:, 1, :], rest[:, :])
                else:
                    ins = dve.tensor_tensor(pieces[:, 2, :], rest[:, :], pieces[:, 1, :], ALU.subtract)
                ins.then_inc(split, 1)

            def z0(c, zg, slot, g, first=False):
                if not first:
                    dve.wait_ge(multiplied, zg - ZSLOTS + 1)
                dve.wait_ge(sel_ready, SELS * c + g + 1)
                if g == 0:
                    dve.wait_ge(sel_copied, COPIES * c + 1)
                    dve.tensor_tensor(z[0:R0_LAST, slot, 0, :], selp[0:R0_LAST, 0, 1, :], xdup[0:R0_LAST, :],
                                      ALU.mult).then_inc(z_ready, 1)
                else:
                    dve.tensor_tensor(z[0:R0, slot, :, :], selp[0:R0, g % 2, :, :],
                                      xdup[:, :].unsqueeze(1).broadcast_to([R0, 2, N]), ALU.mult).then_inc(z_ready, 1)

            def z12(h, s, q, phase, g, last):
                wait_past(dve, multiplied, zi(s, phase, g, last) - ZSLOTS + 1)
                dve.tensor_tensor(z[:, zslot(q, phase, g, last), :, :], xb[:, 2 * g:2 * g + 2, :],
                                  h[:, :].unsqueeze(1).broadcast_to([128, 2, N]), ALU.mult).then_inc(z_ready, 1)

            for i in range(4):
                split_step(0, i, first=True)
            for g in range(G0):
                z0(0, g, g, g, first=True)

            def step(bt, q, last):
                s = bt * CPB + q
                dve.wait_ge(h_ready[0], 2 * (s + 1))
                for g in range(XPAIRS):
                    dve.wait_ge(sel_copied, COPIES * s + 1 + g + 1)
                    z12(h1, s, q, "L1", g, last)
                if q == 2 and more(bt):
                    for i in range(4):
                        split_step(bt + 1, i)
                if not last:
                    for g in range(G0):
                        z0(s + 1, zi(s, "L0", g), zslot(q, "L0", g), g)
                dve.wait_ge(h_ready[1], 2 * (s + 1))
                for g in range(XPAIRS):
                    z12(h2, s, q, "L2", g, last)

            steps(dve, step)

        @block.tensor
        def _(pe):
            pe.wait_ge(const_in, 16 * N_CONST)

            def turn(bt, hf):
                pe.wait_ge(split, 4 * (bt + 1))
                wait_past(pe, xs_ready, 2 * bt + hf)
                pv = pieces[:, :, :].rearrange("p a (f d) -> p d (a f)", d=D)
                for k in range(D // 2):
                    last = pe.transpose(turned[0:KS, k * BT:(k + 1) * BT], pv[:, hf * (D // 2) + k, :], ident_sb[:, :])
                last.then_inc(turned_ready, 1)

            def select(c, q, p, first=False):
                if p < 2:
                    if not first:
                        pe.wait_ge(sel_copied, COPIES * c - 1 + p)
                elif p < G0 + 2:
                    if p == 2:
                        pe.wait_ge(sel_copied, COPIES * c + 1)
                    pe.wait_ge(z_ready, GROUPS * c + (0 if first else XPAIRS + G0 - GROUPS) + p - 1)
                else:
                    pe.wait_ge(sel_copied, COPIES * c + 1 + p - G0 - 1)
                cols = xs[:, q % CPB * N:(q % CPB + 1) * N]
                if p < G0:
                    tiles = [T0] + layer0_tiles(0) if p == 0 else layer0_tiles(p)
                    for i, t in enumerate(tiles):
                        ins = pe.matmul(selp[0:R0, p % 2, i, :], sel0_sb[:, t, :], cols, start=True, stop=True)
                else:
                    for i in range(2):
                        ins = pe.matmul(selp[:, p % 2, i, :], selx_sb[:, 2 * (p - G0) + i, :], cols, start=True, stop=True)
                ins.then_inc(sel_ready, 1)

            def layer0(c, zg, slot, g, first=False):
                if g == 0 and not first:
                    pe.wait_ge(h_ready[0], 2 * c)
                    pe.wait_ge(dir_ready[0], c)
                pe.wait_ge(z_ready, zg + 1)
                for i, t in enumerate(layer0_tiles(g)):
                    rows = R0_LAST if t == T0 - 1 else R0
                    ins = pe.matmul(acc0[:, :], w0_sb[0:rows, t, :], z[0:rows, slot, i, :],
                                    start=(g == 0), stop=(g == G0 - 1 and i == 1))
                ins.then_inc(multiplied, 1)

            def layer12(acc, w, zg, slot, g):
                pe.wait_ge(z_ready, zg + 1)
                for i in range(2):
                    t = 2 * g + i
                    rows = H if t == T1 - 1 else 128
                    ins = pe.matmul(acc[:, :], w[0:rows, t, :], z[0:rows, slot, i, :], start=(t == 0), stop=(t == T1 - 1))
                ins.then_inc(multiplied, 1)

            turn(0, 0)
            turn(0, 1)
            pe.wait_ge(xs_ready, 1)
            pe.wait_ge(w0_ready, 2)
            for p in range(G0):
                select(0, 0, p, first=True)
            for p in range(G0, SELS):
                select(0, 0, p, first=True)
            for g in range(G0):
                layer0(0, g, g, g, first=True)

            def step(bt, q, last):
                s = bt * CPB + q
                nq = q + 1
                if not last and nq in (2, CPB):
                    pe.wait_ge(xs_ready, 2 * bt + (2 if nq == 2 else 3))
                wait_past(pe, h_ready[1], 2 * s)
                wait_past(pe, dir_ready[1], s)
                for g in range(XPAIRS):
                    layer12(acc1, w1_sb, zi(s, "L1", g, last), zslot(q, "L1", g, last), g)
                    if not last and g in (3, 4, 7, 9):
                        select(s + 1, nq, (3, 4, 7, 9).index(g))
                if not last:
                    for g in range(G0):
                        layer0(s + 1, zi(s, "L0", g), zslot(q, "L0", g), g)
                wait_past(pe, dir_ready[2], s)
                for g in range(XPAIRS):
                    layer12(acc2, w2_sb, zi(s, "L2", g, last), zslot(q, "L2", g, last), g)
                    if not last:
                        select(s + 1, nq, G0 + g)
                        if g == 6 and q >= 2 and more(bt):
                            turn(bt + 1, q - 2)

            steps(pe, step)

            pe.wait_ge(folded, 4 * NBT)
            na = 0
            per = M_TOP1 // 128 + M_TOP2 // 128
            for nh in range(B // N):
                cols = slice(nh * N, (nh + 1) * N)
                for m in range(M_TOP1 // 128):
                    ms = slice(m * 128, (m + 1) * 128)
                    acc = [acc0, acc1, acc2][m % 3]
                    if nh == 0 and m == 0:
                        pe.wait_ge(dir_ready[2], NCHUNK)
                    if nh > 0 and m < 3:
                        pe.wait_ge(top_act, per * nh)
                    if m == 3:
                        pe.wait_ge(top_act, per * nh + 1)
                    pe.matmul(acc[:, :], wt1_sb[:, 0, ms], feat[:, 0, cols], start=True, stop=False)
                    pe.matmul(acc[:, :], wt1_sb[:, 1, ms], feat[:, 1, cols], start=False, stop=False)
                    pe.matmul(acc[:, :], wt1d_sb[:, ms], dense_sb[:, cols], start=False, stop=True).then_inc(top_acc, 1)
                pe.wait_ge(top_act, per * nh + M_TOP1 // 128)
                for m in range(M_TOP2 // 128):
                    for k in range(M_TOP1 // 128):
                        ins = pe.matmul(selp[:, 0, m, :], wt2_sb[:, k, m * 128:(m + 1) * 128], t1[:, k, :],
                                        start=(k == 0), stop=(k == M_TOP1 // 128 - 1))
                    ins.then_inc(top_acc, 1)
                pe.wait_ge(top_act, per * (nh + 1))
                if nh > 0:
                    pe.wait_ge(y_ready, nh)
                for k in range(M_TOP2 // 128):
                    ins = pe.matmul(selp[0:1, 1, 0, :], cols_sb[:, COL_W3 + k:COL_W3 + k + 1], t2[:, k, :], start=(k == 0), stop=(k == 1))
                ins.then_inc(top_acc, 1)


def shape_constants():
    sel0 = np.zeros((PIECES, F, T0 + 1, SPT, F), np.float32)
    for t in range(T0):
        for k in range(SPT):
            if t * SPT + k < SHIFTS:
                for f in range(F):
                    sel0[:, (f + t * SPT + k) % F, t, k, f] = 1
    for f in range(F):
        sel0[:, f, T0, :, f] = 1
    selx = np.zeros((PIECES, F, F + 1, H), np.float32)
    for f in range(F):
        selx[:, f, f, :] = 1
    bf = np.dtype("bfloat16")
    return (sel0.reshape(KS, T0 + 1, R0).astype(bf), selx.reshape(KS, T1, 2 * H).astype(bf), np.eye(128).astype(bf))


def column_vectors(inputs):
    b0, b1, b2, bt1, bt2, w3 = (np.asarray(inputs[n]).ravel() for n in
                                ("L0_rec_b0", "L0_rec_b1", "L0_rec_b2", "b_top1", "b_top2", "W_top3"))
    rows = [np.concatenate([b[i:i + H]] * 2) for b in (b0, b1) for i in (0, H)] + [b2]
    rows += list(bt1.reshape(-1, 128)) + list(bt2.reshape(-1, 128)) + list(w3.reshape(-1, 128))
    return np.ascontiguousarray(np.stack(rows).T)


def kernel(**inputs):
    import concourse.bacc as bacc
    from concourse.bass_utils import run_bass_kernel_spmd

    nc = bacc.Bacc("TRN2", target_bir_lowering=False, num_devices=1)
    sel0, selx, ident = shape_constants()
    w0 = np.asarray(inputs["L0_rec_W0"])
    f = np.arange(F)[None, :]
    g = (f + np.arange(SHIFTS)[:, None]) % F
    arrays = {"dense_t": np.ascontiguousarray(np.asarray(inputs["dense_ctx"]).T), "ids": np.asarray(inputs["ids"])}
    for i in range(F):
        arrays[f"tbl_{i}"] = np.asarray(inputs[f"tbl_{i}"])
    arrays.update(
        w0_fwd=np.ascontiguousarray(w0[(f * F + g).ravel()]), w0_rev=np.ascontiguousarray(w0[(g * F + f).ravel()]),
        w1=np.asarray(inputs["L0_rec_W1"]), w2=np.asarray(inputs["L0_rec_W2"]), wt1=np.asarray(inputs["W_top1"]),
        wt2=np.asarray(inputs["W_top2"]), columns=column_vectors(inputs), sel0=sel0, selx=selx, ident=ident)
    aps = {name: nc.dram_tensor(f"in_{name}", a.shape, mybir.dt.from_np(a.dtype), kind="ExternalInput").ap()
           for name, a in arrays.items()}
    out = nc.dram_tensor("out_y", (1, B), FP32, kind="ExternalOutput").ap()
    tables = [aps.pop(f"tbl_{i}") for i in range(F)]
    build(nc, tables=tables, out=out, **aps)
    r = run_bass_kernel_spmd(nc, [{f"in_{name}": a for name, a in arrays.items()}], core_ids=[0])
    return np.asarray(r.results[0]["out_y"]).reshape(B, 1)
```

```python
from contextlib import ExitStack

import numpy as np
import concourse.bass as bass
from concourse import mybir

FP32 = mybir.dt.float32
FP32R = mybir.dt.float32r
BF16 = mybir.dt.bfloat16
ALU = mybir.AluOpType
ACT = mybir.ActivationFunctionType

B, F, D = 1024, 39, 16
L, H = 128, 64
BT = 128
NBT = B // BT
N = 512
DQ = N // BT
CPB = D // DQ
NCHUNK = NBT * CPB

SHIFTS = F // 2 + 1
SPT = 128 // F
R0 = SPT * F
T0 = -(-SHIFTS // SPT)
R0_LAST = (SHIFTS - (T0 - 1) * SPT) * F
T1 = -(-F // 2)
XPAIRS = T1 // 2
G0 = T0 // 2 + 1
GROUPS = 2 * XPAIRS + G0
SELS = G0
QUADS = XPAIRS // 2
SPLIT = (1, 3, 5, 7, 8)
WHOLE_RING = 7
SPLIT_RING = 4
WHOLE = tuple(g for g in range(XPAIRS) if g not in SPLIT)
GROUPS_WHOLE = GROUPS - 2 * len(SPLIT)
WAITING = 4
PIECES = 3
KS = PIECES * F

K_TOP = 272
M_TOP1 = 512
M_TOP2 = 256
DENSE = 16
COL_H0, COL_D0, COL_H1, COL_D1, COL_B2 = range(5)
COL_BT1 = 5
COL_BT2 = COL_BT1 + M_TOP1 // 128
COL_W3 = COL_BT2 + M_TOP2 // 128
COLS = COL_W3 + M_TOP2 // 128
ADDS = CPB - 1
LOW_LAG = 2
SPLIT_AT = 4
EVACUATE0_AT = 5
EVACUATE2_AT = 3
TURN_AT = 1
TURN_COPY_AT = 6
L0_AT = (3, 4, 6, 9)
N_CONST = 6 + 2 * (XPAIRS + 1)


def layer0_tiles(g):
    return [T0 - 1] if g == 0 else [2 * g - 2, 2 * g - 1]


def build(nc, dense_t, ids, tables, w0_fwd, w0_rev, w1, w2,
          wt1, wt2, columns, sel0, ident, x_dram, out):
    with ExitStack() as ctx:
        def sb(name, shape, dt=FP32):
            return ctx.enter_context(nc.sbuf_tensor(name, shape, dt))

        def psum(name, shape, dt=FP32):
            return ctx.enter_context(nc.psum_tensor(name, shape, dt))

        def sem(name):
            return ctx.enter_context(nc.semaphore(name))

        idx = sb("idx", [BT, F], mybir.dt.int32)
        emb = sb("emb", [BT, F * D])
        pieces = sb("pieces", [BT, PIECES, F * D], BF16)
        xs = sb("xs", [128, D * BT], BF16)
        w0_sb = sb("w0_sb", [R0, T0, L])
        w12_sb = sb("w12_sb", [128, 2, len(WHOLE), 2, L])
        whigh = sb("whigh", [128, 2, len(SPLIT), 2, L], FP32R)
        wlow = sb("wlow", [128, 2, len(SPLIT), 2, L], FP32R)
        sel0_sb = sb("sel0_sb", [KS, T0 + 1, R0], BF16)
        ident_sb = sb("ident_sb", [128, 128], BF16)
        cols_sb = sb("cols_sb", [128, COLS])
        wt1_sb = sb("wt1_sb", [128, 2, M_TOP1])
        wt1d_sb = sb("wt1d_sb", [DENSE, M_TOP1])
        wt2_sb = xs[:, :].bitcast(FP32).rearrange("p (c m) -> p c m", m=M_TOP2)
        dense_sb = sb("dense_sb", [DENSE, B])
        xdup = sb("xdup", [R0, N])
        xb = sb("xb", [128, T1, N])
        w_stage = xb[:, 0:len(SPLIT), :].rearrange("p k (a t l) -> p a k t l", a=2, t=2)
        h1 = sb("h1", [128, N])
        h2 = sb("h2", [128, N])
        z = sb("z", [128, WHOLE_RING, 2, N])
        zfull = sb("zfull", [128, WAITING, 2, N])
        zhigh = sb("zhigh", [128, SPLIT_RING, 2, N], FP32R)
        zlow = sb("zlow", [128, SPLIT_RING, 2, N], FP32R)
        w0r_sb = zfull[0:R0, 0, :, :].rearrange("p a n -> p (a n)")[:, 0:T0 * L].rearrange("p (t l) -> p t l", l=L)
        dir01 = sb("dir01", [128, 2, N])
        dir2 = sb("dir2", [128, 2, N])
        sum01 = sb("sum01", [128, N])
        sum2 = sb("sum2", [128, N])
        half = sb("half", [128, 2, N // 2])
        feat = sb("feat", [128, 2, B])
        t1 = z[:, 0:2, :, :].rearrange("p a b n -> p (a b) n")
        t2 = z[:, 2, :, :]
        y_sb = xb[0:1, 0:2, :].rearrange("p a n -> p (a n)")

        acc0 = psum("acc0", [128, N])
        acc1 = psum("acc1", [128, N])
        selp = psum("selp", [128, 2, 2, N])
        spare = psum("spare", [128, 2, N])
        acc2 = spare[:, 0, :]
        turned = spare[:, 1, :].bitcast(BF16)

        def pair(p):
            return spare if p == 2 else selp[:, p % 3 % 2, :, :]

        const_in = sem("const_in")
        w0_in = sem("w0_in")
        w0_zeroed = sem("w0_zeroed")
        w0_ready = sem("w0_ready")
        idx_in = sem("idx_in")
        gather_turns = sem("gather_turns")
        gathered = sem("gathered")
        split = sem("split")
        turned_ready = sem("turned_ready")
        xs_ready = sem("xs_ready")
        sel_ready = sem("sel_ready")
        xdup_ready = sem("xdup_ready")
        x_stored = sem("x_stored")
        spread_turns = sem("spread_turns")
        xb_in = [sem(f"xb_in{i}") for i in range(QUADS)]
        pad_zeroed = sem("pad_zeroed")
        z_ready = sem("z_ready")
        full_ready = sem("full_ready")
        high_ready = sem("high_ready")
        low_ready = sem("low_ready")
        w_split = sem("w_split")
        multiplied = sem("multiplied")
        h_ready = [sem(f"h{i + 1}_ready") for i in range(2)]
        dir_ready = [sem(f"dir{i}_ready") for i in range(3)]
        sum01_done = sem("sum01_done")
        sum2_done = sem("sum2_done")
        folded = sem("folded")
        late_in = sem("late_in")
        top_acc = sem("top_acc")
        top_act = sem("top_act")
        y_ready = sem("y_ready")
        y_out = sem("y_out")

        block = ctx.enter_context(nc.Block())

        def zi(s, phase, g, last=False):
            off = {"L1": 0, "L0": XPAIRS, "L2": XPAIRS if last else XPAIRS + G0}[phase]
            return G0 + GROUPS * s + off + g

        kinds = [False] * G0
        for s_ in range(NCHUNK):
            layer12_kinds = [g in SPLIT for g in range(XPAIRS)]
            kinds += layer12_kinds + ([] if s_ == NCHUNK - 1 else [False] * G0) + layer12_kinds
        rank = [sum(k == kinds[i] for k in kinds[:i]) for i in range(len(kinds))]
        place = {(kinds[i], rank[i]): i for i in range(len(kinds))}

        class Group:

            def __init__(self, s, q, phase, g, last=False, first=False):
                ref = s if isinstance(s, int) else CPB + q
                i = g if first else zi(ref, phase, g, last)
                self.split = kinds[i]
                ring = SPLIT_RING if self.split else WHOLE_RING
                self.slot = rank[i] % ring
                self.wait_slot = rank[i] % WAITING
                before = place.get((self.split, rank[i] - ring), -1)
                lap = 0 if isinstance(s, int) else s - ref
                per = kinds[G0:G0 + GROUPS].count(self.split)
                self.count = i + 1 + GROUPS * lap
                self.kind_count = rank[i] + 1 + per * lap
                self.free = before + 1 + GROUPS * lap
                self.wait_free = self.kind_count - WAITING

        assert CPB * GROUPS_WHOLE % WHOLE_RING == 0 and CPB * 2 * len(SPLIT) % SPLIT_RING == 0

        def wait_past(eng, sem, n):
            if not isinstance(n, int) or n > 0:
                eng.wait_ge(sem, n)

        def steps(eng, body):
            for q in range(CPB):
                body(0, q, False)
            with eng.Fori(1, NBT - 1) as bt:
                for q in range(CPB):
                    body(bt, q, False)
            for q in range(CPB):
                body(NBT - 1, q, q == CPB - 1)

        def dir_freed(bt, q):
            return ADDS * bt + (q - 1 if q < 2 else 1)

        def more(bt):
            return not isinstance(bt, int) or bt < NBT - 1

        @block.sync
        def _(sp):
            def load_idx(bt):
                sp.dma_start(idx[:, :], ids[bass.ds(bt * BT, BT), :]).then_inc(idx_in, 16)

            load_idx(0)
            body = (T0 - 1) * R0
            sp.dma_start(w0_sb[:, 0:T0 - 1, :], w0_fwd[0:body, :].rearrange("(t p) l -> p t l", p=R0)).then_inc(w0_in, 16)
            sp.dma_start(w0_sb[0:R0_LAST, T0 - 1, :], w0_fwd[body:body + R0_LAST, :]).then_inc(w0_in, 16)
            sp.wait_ge(w0_zeroed, 1)
            sp.dma_start(w0r_sb[F:R0, 0, :], w0_rev[F:R0, :]).then_inc(w0_in, 16)
            sp.dma_start(w0r_sb[:, 1:T0 - 1, :], w0_rev[R0:body, :].rearrange("(t p) l -> p t l", p=R0)).then_inc(w0_in, 16)
            sp.dma_start(w0r_sb[0:R0_LAST, T0 - 1, :], w0_rev[body:body + R0_LAST, :]).then_inc(w0_in, 16)

            def prefetch(bt):
                sp.wait_ge(gathered, 16 * F * (bt + 1))
                load_idx(bt + 1)

            def store_x(c, q):
                sp.wait_ge(xdup_ready, c + 1)
                sp.dma_start(x_dram[q % 2, :, :], xdup[0:F, :]).then_inc(x_stored, 16)

            def spread_x(c, q, k, used=None):
                if k == 0:
                    sp.wait_ge(x_stored, 16 * (c + 1))
                    sp.sem_inc(spread_turns)
                if used:
                    sp.wait_ge(full_ready if used.split else z_ready, used.kind_count)
                for odd in range(2):
                    tiles = 4 - (odd and k == QUADS - 1)
                    src = x_dram[q % 2, 8 * k + odd:8 * k + odd + 2 * tiles - 1:2, :]
                    sp.dma_start(xb[odd * H:(odd + 1) * H, 4 * k:4 * k + tiles, :],
                                 src.unsqueeze(0).broadcast_to([H, tiles, N])).then_inc(xb_in[k], 16)

            def step(bt, q, last):
                s = bt * CPB + q
                if q == 0 and more(bt):
                    prefetch(bt)
                if not last:
                    store_x(s + 1, q + 1)
                    for k in range(QUADS):
                        spread_x(s + 1, q + 1, k, used=Group(s, q, "L2", 2 * k + 1))

            sp.wait_ge(w_split, 4 * len(SPLIT))
            store_x(0, 0)
            for k in range(QUADS):
                spread_x(0, 0, k)
            steps(sp, step)
            sp.wait_ge(sel_ready, SELS * NCHUNK)
            sp.dma_start(wt2_sb, wt2.rearrange("(c p) m -> p c m", p=128)).then_inc(late_in, 16)
            sp.wait_ge(y_ready, 2)
            sp.dma_start(out, y_sb[:, :]).then_inc(y_out, 16)
            sp.wait_ge(y_out, 16)

        @block.gpsimd
        def _(pool):
            def gather(bt, f0, f1):
                if f0 == 0:
                    pool.wait_ge(idx_in, 16 * (bt + 1))
                    wait_past(pool, split, 4 * bt)
                    if not isinstance(bt, int):
                        pool.sem_inc(gather_turns)
                for f in range(f0, f1):
                    pool.indirect_dma_start(
                        out=emb[:, f * D:(f + 1) * D], out_offset=None, in_=tables[f],
                        in_offset=bass.IndirectOffsetOnAxis(ap=idx[:, f:f + 1], axis=0),
                    ).then_inc(gathered, 16)

            def add_chunk(total, direct, bt, q, done):
                if q > 1:
                    pool.wait_ge(done, ADDS * bt + q - 1)
                pool.tensor_tensor(total[:, :], direct[:, 0, :] if q == 1 else total[:, :], direct[:, q % 2, :],
                                   ALU.add).then_inc(done, 1)

            def step(bt, q, last):
                s = bt * CPB + q
                if q < 2 and more(bt):
                    gather(bt + 1, *((0, F // 2) if q == 0 else (F // 2, F)))
                if q == 0:
                    return
                if q == 1:
                    wait_past(pool, folded, 4 * bt)
                pool.wait_ge(dir_ready[0], s + 1)
                pool.wait_ge(dir_ready[1], s + 1)
                add_chunk(sum01, dir01, bt, q, sum01_done)
                pool.wait_ge(dir_ready[2], s + 1)
                add_chunk(sum2, dir2, bt, q, sum2_done)
                if q == CPB - 1:
                    for i, (total, done) in enumerate(((sum01, sum01_done), (sum2, sum2_done))):
                        pool.wait_ge(done, ADDS * (bt + 1))
                        pool.tensor_tensor(half[:, i, :], total[:, 0:N // 2], total[:, N // 2:N], ALU.add).then_inc(folded, 1)
                    for i in range(2):
                        pool.wait_ge(folded, 1)
                        pool.wait_ge(folded, 4 * bt + 1 + i)
                        pool.tensor_tensor(feat[:, i, bass.ds(bt * BT, BT)], half[:, i, 0:BT], half[:, i, BT:2 * BT],
                                           ALU.add).then_inc(folded, 1)

            gather(0, 0, F)
            steps(pool, step)

        @block.scalar
        def _(act):
            def load(dst, src):
                act.dma_start(dst, src).then_inc(const_in, 16)

            load(ident_sb[:, :], ident)
            load(sel0_sb[:, :, :], sel0)
            load(dense_sb[:, :], dense_t)
            load(cols_sb[:, :], columns)
            for layer, w in enumerate((w1, w2)):
                for g in range(XPAIRS):
                    dst = w_stage[:, layer, SPLIT.index(g), :, :] if g in SPLIT else w12_sb[:, layer, WHOLE.index(g), :, :]
                    if g < XPAIRS - 1:
                        load(dst, w[2 * g * 128:(2 * g + 2) * 128, :].rearrange("(t p) l -> p t l", p=128))
                    else:
                        load(dst[:, 0, :], w[2 * g * 128:(2 * g + 1) * 128, :])
                        load(dst[0:H, 1, :], w[(2 * g + 1) * 128:, :])
            load(wt1_sb[:, :, :], wt1[0:256, :].rearrange("(c p) m -> p c m", p=128))
            load(wt1d_sb[:, :], wt1[256:K_TOP, :])
            act.wait_ge(const_in, 16 * N_CONST)

            def turn_copy(bt, hf):
                act.wait_ge(turned_ready, 2 * bt + hf + 1)
                act.activation(xs[0:KS, hf * 2 * N:(hf + 1) * 2 * N], turned[0:KS, :], ACT.Copy).then_inc(xs_ready, 1)

            def dup_copy(c):
                act.wait_ge(sel_ready, SELS * c + 1)
                wait_past(act, x_stored, 16 * c)
                act.activation(xdup[:, :], selp[0:R0, 0, 0, :], ACT.Copy).then_inc(xdup_ready, 1)

            def high_part(grp):
                act.wait_ge(full_ready, grp.kind_count)
                wait_past(act, multiplied, grp.free)
                act.activation(zhigh[:, grp.slot, :, :], zfull[:, grp.wait_slot, :, :], ACT.Copy).then_inc(high_ready, 1)

            def relu(dst, src, col, rows=slice(0, 128)):
                return act.activation(dst, src, ACT.Relu, bias=cols_sb[rows, col:col + 1])

            def evacuate0(s, nxt, first=False):
                act.wait_ge(multiplied, G0 if first else zi(s, "L0", G0 - 1) + 1)
                for p in (0, H):
                    relu(h1[p:p + H, :], acc0[0:H, :], COL_H0, slice(0, H)).then_inc(h_ready[0], 1)
                wait_past(act, sum01_done, dir_freed(*nxt))
                relu(dir01[0:H, nxt[1] % 2, :], acc0[H:128, :], COL_D0, slice(H, 128)).then_inc(dir_ready[0], 1)

            def evacuate1(s, q):
                act.wait_ge(multiplied, zi(s, "L1", XPAIRS - 1) + 1)
                for p in (0, H):
                    relu(h2[p:p + H, :], acc1[0:H, :], COL_H1, slice(0, H)).then_inc(h_ready[1], 1)
                relu(dir01[H:128, q % 2, :], acc1[H:128, :], COL_D1, slice(H, 128)).then_inc(dir_ready[1], 1)

            def evacuate2(bt, s, q, last):
                act.wait_ge(multiplied, Group(s, q, "L2", XPAIRS - 1, last).count)
                wait_past(act, sum2_done, dir_freed(bt, q))
                relu(dir2[:, q % 2, :], acc2, COL_B2).then_inc(dir_ready[2], 1)

            turn_copy(0, 0)
            turn_copy(0, 1)
            dup_copy(0)
            evacuate0(-1, (0, 0), first=True)

            def step(bt, q, last):
                s = bt * CPB + q
                for g in range(XPAIRS):
                    if g == EVACUATE2_AT and not (isinstance(s, int) and s == 0):
                        evacuate2(bt if q else bt - 1, s - 1, (q - 1) % CPB, False)
                    if g in SPLIT:
                        high_part(Group(s, q, "L1", g, last))
                    if g == 5 and not last:
                        dup_copy(s + 1)
                evacuate1(s, q)
                for g in range(XPAIRS):
                    if g in SPLIT:
                        high_part(Group(s, q, "L2", g, last))
                    if g == EVACUATE0_AT and not last:
                        evacuate0(s, (bt, q + 1) if q < CPB - 1 else (bt + 1, 0))
                    if g == TURN_COPY_AT and q >= 2 and more(bt):
                        turn_copy(bt + 1, q - 2)
                if last:
                    evacuate2(bt, s, q, last)

            steps(act, step)

            na = 0
            for nh in range(B // N):
                for m in range(M_TOP1 // 128):
                    na += 1
                    act.wait_ge(top_acc, na)
                    act.activation(t1[:, m, :], [acc0[:, :], acc1[:, :], acc2][m % 3], ACT.Relu,
                                   bias=cols_sb[:, COL_BT1 + m:COL_BT1 + m + 1]).then_inc(top_act, 1)
                for m in range(M_TOP2 // 128):
                    na += 1
                    act.wait_ge(top_acc, na)
                    act.activation(t2[:, m, :], selp[:, 0, m, :], ACT.Relu,
                                   bias=cols_sb[:, COL_BT2 + m:COL_BT2 + m + 1]).then_inc(top_act, 1)
                na += 1
                act.wait_ge(top_acc, na)
                act.activation(y_sb[:, nh * N:(nh + 1) * N], selp[0:1, 1, 0, :], ACT.Copy).then_inc(y_ready, 1)

        @block.vector
        def _(dve):
            dve.memset(w0r_sb[:, 0, :], 0.0).then_inc(w0_zeroed, 1)
            dve.memset(xb[H:128, T1 - 1, :], 0.0).then_inc(pad_zeroed, 1)
            dve.wait_ge(w0_in, 16 * 5)
            dve.wait_ge(w0_zeroed, 1)
            dve.tensor_tensor(w0_sb[:, 0:T0 - 1, :], w0_sb[:, 0:T0 - 1, :], w0r_sb[:, 0:T0 - 1, :], ALU.add).then_inc(w0_ready, 1)
            dve.tensor_tensor(w0_sb[0:R0_LAST, T0 - 1, :], w0_sb[0:R0_LAST, T0 - 1, :], w0r_sb[0:R0_LAST, T0 - 1, :],
                              ALU.add).then_inc(w0_ready, 1)

            def split_step(bt, i, first=False):
                if i == 0:
                    dve.wait_ge(gathered, 16 * F * (bt + 1))
                    if not first:
                        dve.wait_ge(turned_ready, 2 * bt)
                else:
                    dve.wait_ge(split, 4 * bt + i)
                if i == 0:
                    ins = dve.tensor_copy(pieces[:, 0, :], emb[:, :])
                elif i == 1:
                    ins = dve.tensor_tensor(emb[:, :], emb[:, :], pieces[:, 0, :], ALU.subtract)
                elif i == 2:
                    ins = dve.tensor_copy(pieces[:, 1, :], emb[:, :])
                else:
                    ins = dve.tensor_tensor(pieces[:, 2, :], emb[:, :], pieces[:, 1, :], ALU.subtract)
                ins.then_inc(split, 1)

            def z0(c, g, grp):
                wait_past(dve, multiplied, grp.free)
                dve.wait_ge(sel_ready, SELS * c + g + 1)
                if g == 0:
                    dve.wait_ge(xdup_ready, c + 1)
                    dve.tensor_tensor(z[0:R0_LAST, grp.slot, 0, :], pair(0)[0:R0_LAST, 1, :], xdup[0:R0_LAST, :],
                                      ALU.mult).then_inc(z_ready, 1)
                else:
                    dve.tensor_tensor(z[0:R0, grp.slot, :, :], pair(g)[0:R0, :, :],
                                      xdup[:, :].unsqueeze(1).broadcast_to([R0, 2, N]), ALU.mult).then_inc(z_ready, 1)

            def z12(h, g, grp):
                if grp.split:
                    wait_past(dve, low_ready, grp.wait_free)
                    dst, ready = zfull[:, grp.wait_slot, :, :], full_ready
                else:
                    wait_past(dve, multiplied, grp.free)
                    dst, ready = z[:, grp.slot, :, :], z_ready
                dve.tensor_tensor(dst, xb[:, 2 * g:2 * g + 2, :], h[:, :].unsqueeze(1).broadcast_to([128, 2, N]),
                                  ALU.mult).then_inc(ready, 1)

            def low_part(grp):
                dve.wait_ge(high_ready, grp.kind_count)
                wait_past(dve, multiplied, grp.free)
                dve.tensor_tensor(zlow[:, grp.slot, :, :], zfull[:, grp.wait_slot, :, :],
                                  zhigh[:, grp.slot, :, :].bitcast(FP32), ALU.subtract).then_inc(low_ready, 1)

            def products(h, s, q, phase, last, between=None):
                waiting = []
                for g in range(XPAIRS):
                    if phase == "L1" and g % 2 == 0:
                        dve.wait_ge(xb_in[g // 2], 32 * (s + 1))
                    grp = Group(s, q, phase, g, last)
                    z12(h, g, grp)
                    if waiting and g >= waiting[0][0] + LOW_LAG:
                        low_part(waiting.pop(0)[1])
                    if grp.split:
                        waiting.append((g, grp))
                    if between:
                        between(g)
                for _, grp in waiting:
                    low_part(grp)

            dve.wait_ge(const_in, 16 * N_CONST)
            dve.wait_ge(pad_zeroed, 1)
            for layer in range(2):
                for i in range(len(SPLIT)):
                    dve.tensor_copy(whigh[:, layer, i, :, :], w_stage[:, layer, i, :, :]).then_inc(w_split, 1)
                for i in range(len(SPLIT)):
                    dve.wait_ge(w_split, (2 * layer + 1) * len(SPLIT))
                    dve.tensor_tensor(wlow[:, layer, i, :, :], w_stage[:, layer, i, :, :],
                                      whigh[:, layer, i, :, :].bitcast(FP32), ALU.subtract).then_inc(w_split, 1)
            for i in range(4):
                split_step(0, i, first=True)
            for g in range(G0):
                z0(0, g, Group(0, 0, "L0", g, first=True))

            def step(bt, q, last):
                s = bt * CPB + q
                dve.wait_ge(h_ready[0], 2 * (s + 1))
                products(h1, s, q, "L1", last,
                         between=lambda g: split_step(bt + 1, g - SPLIT_AT)
                         if q == 2 and more(bt) and 0 <= g - SPLIT_AT < 4 else None)
                if not last:
                    for g in range(G0):
                        z0(s + 1, g, Group(s, q, "L0", g))
                dve.wait_ge(h_ready[1], 2 * (s + 1))
                products(h2, s, q, "L2", last)

            steps(dve, step)

        @block.tensor
        def _(pe):
            pe.wait_ge(const_in, 16 * N_CONST)

            def turn(bt, hf):
                pe.wait_ge(split, 4 * (bt + 1))
                wait_past(pe, xs_ready, 2 * bt + hf)
                pv = pieces[:, :, :].rearrange("p a (f d) -> p d (a f)", d=D)
                for k in range(D // 2):
                    last = pe.transpose(turned[0:KS, k * BT:(k + 1) * BT], pv[:, hf * (D // 2) + k, :], ident_sb[:, :])
                last.then_inc(turned_ready, 1)

            def select(c, q, p, used):
                if p == 2:
                    wait_past(pe, dir_ready[2], c - 1)
                if p == 3:
                    pe.wait_ge(xdup_ready, c + 1)
                    pe.wait_ge(z_ready, used.kind_count)
                tiles = [T0] + layer0_tiles(0) if p == 0 else layer0_tiles(p)
                cols = xs[0:KS, q % CPB * N:(q % CPB + 1) * N]
                for i, t in enumerate(tiles):
                    ins = pe.matmul(pair(p)[0:R0, i, :], sel0_sb[:, t, :], cols, start=True, stop=True)
                ins.then_inc(sel_ready, 1)

            def layer0(c, g, grp, first=False):
                if g == 0 and not first:
                    pe.wait_ge(h_ready[0], 2 * c)
                    pe.wait_ge(dir_ready[0], c)
                pe.wait_ge(z_ready, grp.kind_count)
                for i, t in enumerate(layer0_tiles(g)):
                    rows = R0_LAST if t == T0 - 1 else R0
                    ins = pe.matmul(acc0[:, :], w0_sb[0:rows, t, :], z[0:rows, grp.slot, i, :],
                                    start=(g == 0), stop=(g == G0 - 1 and i == 1))
                ins.then_inc(multiplied, 1)

            def layer12(acc, layer, g, grp):
                if grp.split:
                    k = SPLIT.index(g)
                    pe.wait_ge(high_ready, grp.kind_count)
                    for i in range(2):
                        for part in (whigh, wlow):
                            pe.matmul(acc, part[:, layer, k, i, :], zhigh[:, grp.slot, i, :], start=False, stop=False)
                    pe.wait_ge(low_ready, grp.kind_count)
                    for i in range(2):
                        ins = pe.matmul(acc, whigh[:, layer, k, i, :], zlow[:, grp.slot, i, :], start=False, stop=False)
                else:
                    pe.wait_ge(z_ready, grp.kind_count)
                    for i in range(2):
                        t = 2 * g + i
                        rows = H if t == T1 - 1 else 128
                        ins = pe.matmul(acc, w12_sb[0:rows, layer, WHOLE.index(g), i, :], z[0:rows, grp.slot, i, :], start=(t == 0), stop=(t == T1 - 1))
                ins.then_inc(multiplied, 1)

            turn(0, 0)
            turn(0, 1)
            pe.wait_ge(xs_ready, 2)
            pe.wait_ge(w0_ready, 2)
            pe.wait_ge(w_split, 4 * len(SPLIT))
            for p in range(G0):
                select(0, 0, p, used=Group(0, 0, "L0", 0, first=True))
            for g in range(G0):
                layer0(0, g, Group(0, 0, "L0", g, first=True), first=True)

            def step(bt, q, last):
                s = bt * CPB + q
                nq = q + 1
                if not last:
                    pe.wait_ge(xs_ready, 2 * bt + (2 if q < CPB - 1 else 3))
                wait_past(pe, h_ready[1], 2 * s)
                wait_past(pe, dir_ready[1], s)
                for g in range(XPAIRS):
                    layer12(acc1[:, :], 0, g, Group(s, q, "L1", g, last))
                    if not last and g in L0_AT:
                        select(s + 1, nq, L0_AT.index(g), used=Group(s, q, "L0", 0))
                if not last:
                    for g in range(G0):
                        layer0(s + 1, g, Group(s, q, "L0", g))
                wait_past(pe, dir_ready[2], s)
                for g in range(XPAIRS):
                    layer12(acc2, 1, g, Group(s, q, "L2", g, last))
                    if not last:
                        if g == TURN_AT and q >= 2 and more(bt):
                            turn(bt + 1, q - 2)

            steps(pe, step)

            pe.wait_ge(folded, 4 * NBT)
            pe.wait_ge(late_in, 16)
            na = 0
            per = M_TOP1 // 128 + M_TOP2 // 128
            for nh in range(B // N):
                cols = slice(nh * N, (nh + 1) * N)
                for m in range(M_TOP1 // 128):
                    ms = slice(m * 128, (m + 1) * 128)
                    acc = [acc0[:, :], acc1[:, :], acc2][m % 3]
                    if nh == 0 and m == 0:
                        pe.wait_ge(dir_ready[2], NCHUNK)
                    if nh > 0 and m < 3:
                        pe.wait_ge(top_act, per * nh)
                    if m == 3:
                        pe.wait_ge(top_act, per * nh + 1)
                    pe.matmul(acc, wt1_sb[:, 0, ms], feat[:, 0, cols], start=True, stop=False)
                    pe.matmul(acc, wt1_sb[:, 1, ms], feat[:, 1, cols], start=False, stop=False)
                    pe.matmul(acc, wt1d_sb[:, ms], dense_sb[:, cols], start=False, stop=True).then_inc(top_acc, 1)
                pe.wait_ge(top_act, per * nh + M_TOP1 // 128)
                for m in range(M_TOP2 // 128):
                    for k in range(M_TOP1 // 128):
                        ins = pe.matmul(selp[:, 0, m, :], wt2_sb[:, k, m * 128:(m + 1) * 128], t1[:, k, :],
                                        start=(k == 0), stop=(k == M_TOP1 // 128 - 1))
                    ins.then_inc(top_acc, 1)
                pe.wait_ge(top_act, per * (nh + 1))
                if nh > 0:
                    pe.wait_ge(y_ready, nh)
                for k in range(M_TOP2 // 128):
                    ins = pe.matmul(selp[0:1, 1, 0, :], cols_sb[:, COL_W3 + k:COL_W3 + k + 1], t2[:, k, :], start=(k == 0), stop=(k == 1))
                ins.then_inc(top_acc, 1)


def shape_constants():
    sel0 = np.zeros((PIECES, F, T0 + 1, SPT, F), np.float32)
    for t in range(T0):
        for k in range(SPT):
            if t * SPT + k < SHIFTS:
                for f in range(F):
                    sel0[:, (f + t * SPT + k) % F, t, k, f] = 1
    for f in range(F):
        sel0[:, f, T0, :, f] = 1
    bf = np.dtype("bfloat16")
    return (sel0.reshape(KS, T0 + 1, R0).astype(bf), np.eye(128).astype(bf))


def column_vectors(inputs):
    b0, b1, b2, bt1, bt2, w3 = (np.asarray(inputs[n]).ravel() for n in
                                ("L0_rec_b0", "L0_rec_b1", "L0_rec_b2", "b_top1", "b_top2", "W_top3"))
    rows = [np.concatenate([b[i:i + H]] * 2) for b in (b0, b1) for i in (0, H)] + [b2]
    rows += list(bt1.reshape(-1, 128)) + list(bt2.reshape(-1, 128)) + list(w3.reshape(-1, 128))
    return np.ascontiguousarray(np.stack(rows).T)


def kernel(**inputs):
    import concourse.bacc as bacc
    from concourse.bass_utils import run_bass_kernel_spmd

    nc = bacc.Bacc("TRN2", target_bir_lowering=False, num_devices=1)
    sel0, ident = shape_constants()
    w0 = np.asarray(inputs["L0_rec_W0"])
    f = np.arange(F)[None, :]
    g = (f + np.arange(SHIFTS)[:, None]) % F
    arrays = {"dense_t": np.ascontiguousarray(np.asarray(inputs["dense_ctx"]).T), "ids": np.asarray(inputs["ids"])}
    for i in range(F):
        arrays[f"tbl_{i}"] = np.asarray(inputs[f"tbl_{i}"])
    arrays.update(
        w0_fwd=np.ascontiguousarray(w0[(f * F + g).ravel()]), w0_rev=np.ascontiguousarray(w0[(g * F + f).ravel()]),
        w1=np.asarray(inputs["L0_rec_W1"]), w2=np.asarray(inputs["L0_rec_W2"]), wt1=np.asarray(inputs["W_top1"]),
        wt2=np.asarray(inputs["W_top2"]), columns=column_vectors(inputs), sel0=sel0, ident=ident)
    aps = {name: nc.dram_tensor(f"in_{name}", a.shape, mybir.dt.from_np(a.dtype), kind="ExternalInput").ap()
           for name, a in arrays.items()}
    out = nc.dram_tensor("out_y", (1, B), FP32, kind="ExternalOutput").ap()
    x_dram = nc.dram_tensor("x_dram", (2, F, N), FP32, kind="Internal").ap()
    tables = [aps.pop(f"tbl_{i}") for i in range(F)]
    build(nc, tables=tables, x_dram=x_dram, out=out, **aps)
    r = run_bass_kernel_spmd(nc, [{f"in_{name}": a for name, a in arrays.items()}], core_ids=[0])
    return np.asarray(r.results[0]["out_y"]).reshape(B, 1)
```

```python
from contextlib import ExitStack

import numpy as np
import concourse.bass as bass
from concourse import mybir

FP32 = mybir.dt.float32
FP32R = mybir.dt.float32r
ALU = mybir.AluOpType
ACT = mybir.ActivationFunctionType

B, F, D = 1024, 39, 16
L, H = 128, 64
BT = 128
NBT = B // BT
N = 512
DQ = N // BT
CPB = D // DQ
NCHUNK = NBT * CPB

SHIFTS = F // 2 + 1
SPT = 128 // F
R0 = SPT * F
T0 = -(-SHIFTS // SPT)
R0_LAST = (SHIFTS - (T0 - 1) * SPT) * F
T1 = -(-F // 2)
XPAIRS = T1 // 2
PER0 = 3
G0 = 1 + (T0 - 1) // PER0
GROUPS = 2 * XPAIRS + G0
QUADS = XPAIRS // 2
SPLIT_GROUPS = ((2, 4, 6, 8), (2, 4, 6, 8))
WHOLE_RING = 4
SPLIT_RING = 4
SPLIT = tuple((layer, g) for layer in range(2) for g in SPLIT_GROUPS[layer])
WHOLE = tuple((layer, g) for layer in range(2) for g in range(XPAIRS) if (layer, g) not in SPLIT)
WAITING = 4

K_TOP = 272
M_TOP1 = 512
M_TOP2 = 256
DENSE = 16
COL_H0, COL_D0, COL_H1, COL_D1, COL_B2 = range(5)
COL_BT1 = 5
COL_BT2 = COL_BT1 + M_TOP1 // 128
COL_W3 = COL_BT2 + M_TOP2 // 128
COLS = COL_W3 + M_TOP2 // 128
ADDS = CPB - 1
EARLY = 30
LOW_LAG = 2
EVACUATE0_AT = 5
EVACUATE2_AT = 3
COPY_AT = (2, 4, 6)
TOP_AT = ((0, "L2", 1), (1, "L2", 1), (2, "L1", 0))
TOP_ACT_AT = ((0, "L2", 6), (1, "L2", 6), (2, "L1", 4))
SELECT_AT = 3
DUP_AT = 7
STORE_AT = 3
SHIFT_AT = 4
Z0_AT = XPAIRS
N_CONST = 6 + 2 * (XPAIRS + 2)


def layer0_tiles(g):
    return [T0 - 1] if g == 0 else list(range(PER0 * (g - 1), PER0 * g))


def build(nc, dense_t, ids, tables, w0_fwd, w0_rev, w1, w2,
          wt1, wt2, columns, ident, x_dram, out):
    with ExitStack() as ctx:
        def sb(name, shape, dt=FP32):
            return ctx.enter_context(nc.sbuf_tensor(name, shape, dt))

        def psum(name, shape, dt=FP32):
            return ctx.enter_context(nc.psum_tensor(name, shape, dt))

        def sem(name):
            return ctx.enter_context(nc.semaphore(name))

        idx = sb("idx", [BT, F], mybir.dt.int32)
        emb = sb("emb", [BT, F * D])
        rows = sb("rows", [BT, D, SPT, F])
        w0_sb = sb("w0_sb", [R0, T0, L])
        w12_sb = sb("w12_sb", [128, len(WHOLE), 2, L])
        whigh = sb("whigh", [128, len(SPLIT), 2, L], FP32R)
        wlow = sb("wlow", [128, len(SPLIT), 2, L], FP32R)
        ident_sb = sb("ident_sb", [128, 128])
        wlast_sb = sb("wlast_sb", [128, 2, L])
        wlast_high = sb("wlast_high", [128, 2, L], FP32R)
        wlast_low = sb("wlast_low", [H, 2, L], FP32R)
        cols_sb = sb("cols_sb", [128, COLS])
        wt1_sb = sb("wt1_sb", [128, 2, M_TOP1])
        wt1d_sb = sb("wt1d_sb", [DENSE, M_TOP1])
        wt2_sb = sb("wt2_sb", [128, M_TOP1 // 128, M_TOP2])
        dense_sb = sb("dense_sb", [DENSE, B])
        xdup = sb("xdup", [R0, N])
        z0 = sb("z0", [R0, T0, N])
        xb = sb("xb", [128, T1, N])
        w_stage = xb[:, 0:-(-len(SPLIT) // 2), :].rearrange("p c (k t l) -> p (c k) t l", k=2, t=2)
        h1 = sb("h1", [128, N])
        h2 = sb("h2", [128, N])
        z = sb("z", [128, WHOLE_RING, 2, N])
        zfull = sb("zfull", [128, WAITING, 2, N])
        zhigh = sb("zhigh", [128, SPLIT_RING, 2, N], FP32R)
        zlow = sb("zlow", [128, SPLIT_RING, 2, N], FP32R)
        zlast = sb("zlast", [128, N], FP32R)
        w0r_sb = zfull[0:R0, 0, :, :].rearrange("p a n -> p (a n)")[:, 0:T0 * L].rearrange("p (t l) -> p t l", l=L)
        dir01 = sb("dir01", [128, 2, N])
        dir2 = sb("dir2", [128, 2, N])
        sum01 = sb("sum01", [128, N])
        sum2 = sb("sum2", [128, N])
        half = sb("half", [128, 2, N // 2])
        feat = sb("feat", [128, 2, BT])
        t1 = sb("t1", [128, M_TOP1 // 128, BT])
        t2 = sb("t2", [128, M_TOP2 // 128, BT])
        y_sb = dense_sb[0:1, :]

        acc0 = psum("acc0", [128, N])
        acc1 = psum("acc1", [128, N])
        acc2 = psum("acc2", [128, N])
        dup = psum("dup", [R0, N])
        last_top = psum("last_top", [128, M_TOP2 // 128, N])
        top = psum("top", [128, M_TOP1 // 128, BT])

        const_in = sem("const_in")
        w0_in = sem("w0_in")
        w0_zeroed = sem("w0_zeroed")
        w0_ready = sem("w0_ready")
        idx_in = sem("idx_in")
        gather_turns = sem("gather_turns")
        early_gathered = sem("early_gathered")
        gathered = sem("gathered")
        early_copied = sem("early_copied")
        copied = sem("copied")
        sel_ready = sem("sel_ready")
        xdup_ready = sem("xdup_ready")
        x_stored = sem("x_stored")
        spread_turns = sem("spread_turns")
        xb_in = [sem(f"xb_in{i}") for i in range(QUADS)]
        shifted_in = sem("shifted_in")
        z0_ready = sem("z0_ready")
        z_ready = sem("z_ready")
        full_ready = sem("full_ready")
        high_ready = sem("high_ready")
        low_ready = sem("low_ready")
        last_high = sem("last_high")
        last_low = sem("last_low")
        w_split = sem("w_split")
        multiplied = sem("multiplied")
        h_ready = [sem(f"h{i + 1}_ready") for i in range(2)]
        dir_ready = [sem(f"dir{i}_ready") for i in range(3)]
        sum01_done = sem("sum01_done")
        sum2_done = sem("sum2_done")
        last_folded = sem("last_folded")
        folded = sem("folded")
        top_sum = [sem(f"top{i + 1}_sum") for i in range(3)]
        top_ready = [sem(f"top{i + 1}_ready") for i in range(3)]
        y_out = sem("y_out")

        block = ctx.enter_context(nc.Block())

        def zi(s, phase, g, last=False):
            off = {"L1": 0, "L0": XPAIRS, "L2": XPAIRS if last else XPAIRS + G0}[phase]
            return G0 + GROUPS * s + off + g

        kinds = ["layer 0"] * G0
        for s_ in range(NCHUNK):
            layer1_kinds, layer2_kinds = (["split" if (layer, g) in SPLIT else "whole" for g in range(XPAIRS)]
                                          for layer in range(2))
            kinds += layer1_kinds + ([] if s_ == NCHUNK - 1 else ["layer 0"] * G0) + layer2_kinds
        rank = [sum(k == kinds[i] for k in kinds[:i]) for i in range(len(kinds))]
        place = {(kinds[i], rank[i]): i for i in range(len(kinds))}

        class Group:

            def __init__(self, s, q, phase, g, last=False, first=False):
                ref = s if isinstance(s, int) else CPB + q
                i = g if first else zi(ref, phase, g, last)
                self.split = kinds[i] == "split"
                ring = SPLIT_RING if self.split else WHOLE_RING
                self.slot = rank[i] % ring
                self.wait_slot = rank[i] % WAITING
                before = place.get((kinds[i], rank[i] - ring), -1)
                lap = 0 if isinstance(s, int) else s - ref
                per = kinds[G0:G0 + GROUPS].count(kinds[i])
                self.count = i + 1 + GROUPS * lap
                self.kind_count = rank[i] + 1 + per * lap
                self.free = before + 1 + GROUPS * lap
                self.wait_free = self.kind_count - WAITING

        assert CPB * len(WHOLE) % WHOLE_RING == CPB * len(SPLIT) % SPLIT_RING == CPB * len(SPLIT) % WAITING == 0

        def wait_past(eng, sem, n):
            if not isinstance(n, int) or n > 0:
                eng.wait_ge(sem, n)

        def steps(eng, body):
            for q in range(CPB):
                body(0, q, False)
            with eng.Fori(1, NBT - 1) as bt:
                for q in range(CPB):
                    body(bt, q, False)
            for q in range(CPB):
                body(NBT - 1, q, q == CPB - 1)

        def dir_freed(bt, q):
            return ADDS * bt + (q - 1 if q < 2 else 1)

        def more(bt):
            return not isinstance(bt, int) or bt < NBT - 1

        def two_more(bt, q):
            return q < CPB - 2 or more(bt)

        def gathers(bt):
            return 16 * (F * (bt + 1) - EARLY)

        def top_bank(i, m, final):
            if not final or i == 2:
                return top[:, m, :]
            if (i, m) == (0, 0):
                return top[:, 0, :]
            return ((None, acc0, acc1, acc2) if i == 0 else (last_top[:, 0, :], last_top[:, 1, :]))[m][:, 0:BT]

        def first_tile(bt):
            return isinstance(bt, int) and bt == 0

        @block.sync
        def _(sp):
            def load_idx(bt):
                sp.dma_start(idx[:, :], ids[bass.ds(bt * BT, BT), :]).then_inc(idx_in, 16)

            load_idx(0)
            body = (T0 - 1) * R0
            sp.dma_start(w0_sb[:, 0:T0 - 1, :], w0_fwd[0:body, :].rearrange("(t p) l -> p t l", p=R0)).then_inc(w0_in, 16)
            sp.dma_start(w0_sb[0:R0_LAST, T0 - 1, :], w0_fwd[body:body + R0_LAST, :]).then_inc(w0_in, 16)
            sp.wait_ge(w0_zeroed, 1)
            sp.dma_start(w0r_sb[F:R0, 0, :], w0_rev[F:R0, :]).then_inc(w0_in, 16)
            sp.dma_start(w0r_sb[:, 1:T0 - 1, :], w0_rev[R0:body, :].rearrange("(t p) l -> p t l", p=R0)).then_inc(w0_in, 16)
            sp.dma_start(w0r_sb[0:R0_LAST, T0 - 1, :], w0_rev[body:body + R0_LAST, :]).then_inc(w0_in, 16)

            def prefetch(bt):
                sp.wait_ge(gathered, gathers(bt))
                load_idx(bt + 1)

            def store_x(c, q):
                sp.wait_ge(xdup_ready, c + 1)
                sp.dma_start(x_dram[q % 2, :, :], xdup[0:2 * F, :]).then_inc(x_stored, 16)

            def shift_x(c, q, used=None):
                sp.wait_ge(x_stored, 16 * (c + 1))
                sp.sem_inc(spread_turns)
                if used:
                    sp.wait_ge(multiplied, used.count)
                for k in range(SPT):
                    tiles = (SHIFTS - k + SPT - 1) // SPT
                    src = bass.AP(tensor=x_dram.tensor, offset=(q % 2 * 2 * F + k) * N,
                                  ap=[[N, F], [SPT * N, tiles], [1, N]])
                    sp.dma_start(z0[k * F:(k + 1) * F, 0:tiles, :], src).then_inc(shifted_in, 16)

            def spread_x(c, q, k, used=None):
                if used:
                    sp.wait_ge(full_ready if used.split else z_ready, used.kind_count)
                for odd in range(2):
                    tiles = 4 - (odd and k == QUADS - 1)
                    src = x_dram[q % 2, 8 * k + odd:8 * k + odd + 2 * tiles - 1:2, :]
                    sp.dma_start(xb[odd * H:(odd + 1) * H, 4 * k:4 * k + tiles, :],
                                 src.unsqueeze(0).broadcast_to([H, tiles, N])).then_inc(xb_in[k], 16)
                if k == QUADS - 1:
                    sp.dma_start(xb[H:128, T1 - 1, :],
                                 x_dram[q % 2, F - 1, :].unsqueeze(0).broadcast_to([H, N])).then_inc(xb_in[k], 16)

            def step(bt, q, last):
                s = bt * CPB + q
                if q == 0 and more(bt):
                    prefetch(bt)
                if not last:
                    for k in range(QUADS):
                        if k == STORE_AT and two_more(bt, q):
                            store_x(s + 2, q)
                        if k == SHIFT_AT and two_more(bt, q):
                            shift_x(s + 2, q, used=Group(s, q, "L0", G0 - 1))
                        spread_x(s + 1, q + 1, k, used=Group(s, q, "L2", 2 * k + 1))

            store_x(0, 0)
            shift_x(0, 0)
            sp.wait_ge(w_split, 2 + 2 * len(SPLIT))
            for k in range(QUADS):
                spread_x(0, 0, k)
            store_x(1, 1)
            shift_x(1, 1, used=Group(0, 0, "L0", G0 - 1, first=True))
            steps(sp, step)
            sp.wait_ge(top_ready[2], NBT)
            sp.dma_start(out, y_sb).then_inc(y_out, 16)
            sp.wait_ge(y_out, 16)

        @block.gpsimd
        def _(pool):
            def gather(bt, f0, f1):
                if f0 == 0:
                    pool.wait_ge(idx_in, 16 * (bt + 1))
                    wait_past(pool, copied, SPT * bt)
                    if not isinstance(bt, int):
                        pool.sem_inc(gather_turns)
                for f in range(f0, f1):
                    pool.indirect_dma_start(
                        out=emb[:, f * D:(f + 1) * D], out_offset=None, in_=tables[f],
                        in_offset=bass.IndirectOffsetOnAxis(ap=idx[:, f:f + 1], axis=0),
                    ).then_inc(early_gathered if first_tile(bt) and f < EARLY else gathered, 16)

            def add_chunk(total, direct, bt, q, done):
                if q > 1:
                    pool.wait_ge(done, ADDS * bt + q - 1)
                pool.tensor_tensor(total[:, :], direct[:, 0, :] if q == 1 else total[:, :], direct[:, q % 2, :],
                                   ALU.add).then_inc(done, 1)

            def fold(bt, i, total, done):
                pool.wait_ge(done, ADDS * (bt + 1))
                pool.tensor_tensor(half[:, i, :], total[:, 0:N // 2], total[:, N // 2:N], ALU.add).then_inc(folded, 1)
                wait_past(pool, top_sum[0], bt)
                pool.wait_ge(folded, 4 * bt + 2 * i + 1)
                pool.tensor_tensor(feat[:, i, :], half[:, i, 0:BT], half[:, i, BT:2 * BT], ALU.add).then_inc(folded, 1)

            def step(bt, q, last):
                s = bt * CPB + q
                if q < 2 and more(bt):
                    gather(bt + 1, *((0, F // 2) if q == 0 else (F // 2, F)))
                if q == 0:
                    return
                if q == 1:
                    wait_past(pool, folded, 4 * bt)
                pool.wait_ge(dir_ready[0], s + 1)
                pool.wait_ge(dir_ready[1], s + 1)
                add_chunk(sum01, dir01, bt, q, sum01_done)
                if q == CPB - 1:
                    fold(bt, 0, sum01, sum01_done)
                if not last:
                    pool.wait_ge(dir_ready[2], s + 1)
                    add_chunk(sum2, dir2, bt, q, sum2_done)
                    if q == CPB - 1:
                        fold(bt, 1, sum2, sum2_done)

            gather(0, 0, F)
            steps(pool, step)

        @block.scalar
        def _(act):
            def load(dst, src):
                act.dma_start(dst, src).then_inc(const_in, 16)

            load(ident_sb[:, :], ident)
            load(dense_sb[:, :], dense_t)
            load(cols_sb[:, :], columns)
            for layer, w in enumerate((w1, w2)):
                for g in range(XPAIRS):
                    dst = (w_stage[:, SPLIT.index((layer, g)), :, :] if (layer, g) in SPLIT else
                           w12_sb[:, WHOLE.index((layer, g)), :, :])
                    if g < XPAIRS - 1:
                        load(dst, w[2 * g * 128:(2 * g + 2) * 128, :].rearrange("(t p) l -> p t l", p=128))
                    else:
                        load(dst[:, 0, :], w[2 * g * 128:(2 * g + 1) * 128, :])
                        for copy in range(2):
                            load(wlast_sb[copy * H:(copy + 1) * H, layer, :], w[(2 * g + 1) * 128:, :])
            load(wt1_sb[:, :, :], wt1[0:256, :].rearrange("(c p) m -> p c m", p=128))
            load(wt1d_sb[:, :], wt1[256:K_TOP, :])
            load(wt2_sb[:, :, :], wt2.rearrange("(c p) m -> p c m", p=128))
            act.wait_ge(const_in, 16 * N_CONST)

            def copy_rows(bt, k, fields=slice(0, F), done=copied):
                if k == 0:
                    if done is early_copied:
                        act.wait_ge(early_gathered, 16 * EARLY)
                    else:
                        act.wait_ge(gathered, gathers(bt))
                    wait_past(act, sel_ready, CPB * bt)
                act.activation(rows[:, :, k, fields], emb[:, :].rearrange("p (f d) -> p d f", d=D)[:, :, fields],
                               ACT.Copy).then_inc(done, 1)

            def dup_copy(c):
                act.wait_ge(sel_ready, c + 1)
                wait_past(act, x_stored, 16 * c)
                act.activation(xdup[:, :], dup[:, :], ACT.Copy).then_inc(xdup_ready, 1)

            def high_part(grp):
                act.wait_ge(full_ready, grp.kind_count)
                wait_past(act, multiplied, grp.free)
                act.activation(zhigh[:, grp.slot, :, :], zfull[:, grp.wait_slot, :, :], ACT.Copy).then_inc(high_ready, 1)

            def high_last(s, q, phase, last):
                grp = Group(s, q, phase, XPAIRS - 1, last)
                act.wait_ge(z_ready, grp.kind_count)
                if phase == "L2":
                    act.wait_ge(multiplied, Group(s, q, "L1", XPAIRS - 1).count)
                elif not (isinstance(s, int) and s == 0):
                    act.wait_ge(multiplied, Group(s - 1, q - 1, "L2", XPAIRS - 1).count)
                act.activation(zlast[:, :], z[:, grp.slot, 1, :], ACT.Copy).then_inc(last_high, 1)

            def relu(dst, src, col, rows=slice(0, 128)):
                return act.activation(dst, src, ACT.Relu, bias=cols_sb[rows, col:col + 1])

            def evacuate0(s, nxt, first=False):
                act.wait_ge(multiplied, G0 if first else zi(s, "L0", G0 - 1) + 1)
                for p in (0, H):
                    relu(h1[p:p + H, :], acc0[0:H, :], COL_H0, slice(0, H)).then_inc(h_ready[0], 1)
                wait_past(act, sum01_done, dir_freed(*nxt))
                relu(dir01[0:H, nxt[1] % 2, :], acc0[H:128, :], COL_D0, slice(H, 128)).then_inc(dir_ready[0], 1)

            def evacuate1(s, q):
                act.wait_ge(multiplied, zi(s, "L1", XPAIRS - 1) + 1)
                for p in (0, H):
                    relu(h2[p:p + H, :], acc1[0:H, :], COL_H1, slice(0, H)).then_inc(h_ready[1], 1)
                relu(dir01[H:128, q % 2, :], acc1[H:128, :], COL_D1, slice(H, 128)).then_inc(dir_ready[1], 1)

            def evacuate2(bt, s, q, last):
                act.wait_ge(multiplied, Group(s, q, "L2", XPAIRS - 1, last).count)
                wait_past(act, sum2_done, dir_freed(bt, q))
                relu(dir2[:, q % 2, :], acc2[:, :], COL_B2).then_inc(dir_ready[2], 1)

            def top_act(i, bt, final=False):
                if i == 2:
                    act.wait_ge(top_sum[i], 1)
                    act.wait_ge(top_sum[i], bt + 1)
                    act.activation(y_sb[:, bass.ds(bt * BT, BT)], top[0:1, 0, :], ACT.Copy).then_inc(top_ready[2], 1)
                else:
                    act.wait_ge(top_sum[i], bt + 1)
                    dst, col = ((t1, COL_BT1), (t2, COL_BT2))[i]
                    for m in range(dst.shape[1]):
                        if final and m > 0:
                            act.wait_ge(top_sum[i], bt + 1 + m)
                        ins = relu(dst[:, m, :], top_bank(i, m, final), col + m)
                        if final:
                            ins.then_inc(top_ready[i], 1)
                    if not final:
                        ins.then_inc(top_ready[i], 1)

            relu(h1[:, 0:1], cols_sb[:, COL_H0:COL_H0 + 1], COL_H0)
            for k in range(SPT):
                copy_rows(0, k, slice(0, EARLY), early_copied)
            for k in range(SPT):
                copy_rows(0, k, slice(EARLY, F))
            dup_copy(0)
            evacuate0(-1, (0, 0), first=True)
            dup_copy(1)

            def step(bt, q, last):
                s = bt * CPB + q
                for g in range(XPAIRS):
                    if g == EVACUATE2_AT and not (isinstance(s, int) and s == 0):
                        evacuate2(bt if q else bt - 1, s - 1, (q - 1) % CPB, False)
                    if g in SPLIT_GROUPS[0]:
                        high_part(Group(s, q, "L1", g, last))
                    if q == 2 and more(bt) and g in COPY_AT:
                        copy_rows(bt + 1, COPY_AT.index(g))
                    if not first_tile(bt) and (q, "L1", g) in TOP_ACT_AT:
                        top_act(TOP_ACT_AT.index((q, "L1", g)), bt - 1)
                high_last(s, q, "L1", last)
                evacuate1(s, q)
                for g in range(XPAIRS):
                    if g in SPLIT_GROUPS[1]:
                        high_part(Group(s, q, "L2", g, last))
                    if g == EVACUATE0_AT and not last:
                        evacuate0(s, (bt, q + 1) if q < CPB - 1 else (bt + 1, 0))
                    if g == DUP_AT and two_more(bt, q):
                        dup_copy(s + 2)
                    if not first_tile(bt) and (q, "L2", g) in TOP_ACT_AT:
                        top_act(TOP_ACT_AT.index((q, "L2", g)), bt - 1)
                high_last(s, q, "L2", last)
                if last:
                    evacuate2(bt, s, q, last)

            steps(act, step)

            for i in range(3):
                top_act(i, NBT - 1, final=True)

        @block.vector
        def _(dve):
            dve.memset(w0r_sb[:, 0, :], 0.0).then_inc(w0_zeroed, 1)
            dve.wait_ge(w0_in, 16 * 5)
            dve.wait_ge(w0_zeroed, 1)
            dve.tensor_tensor(w0_sb[:, 0:T0 - 1, :], w0_sb[:, 0:T0 - 1, :], w0r_sb[:, 0:T0 - 1, :], ALU.add).then_inc(w0_ready, 1)
            dve.tensor_tensor(w0_sb[0:R0_LAST, T0 - 1, :], w0_sb[0:R0_LAST, T0 - 1, :], w0r_sb[0:R0_LAST, T0 - 1, :],
                              ALU.add).then_inc(w0_ready, 1)

            def products0(c):
                dve.wait_ge(xdup_ready, c + 1)
                dve.wait_ge(shifted_in, 16 * SPT * (c + 1))
                for g in range(G0):
                    t = layer0_tiles(g)
                    rows = R0_LAST if g == 0 else R0
                    tiles = z0[0:rows, t[0]:t[-1] + 1, :]
                    dve.tensor_tensor(tiles, tiles, xdup[0:rows, :].unsqueeze(1).broadcast_to([rows, len(t), N]),
                                      ALU.mult).then_inc(z0_ready, 1)

            def z12(h, g, grp):
                if grp.split:
                    wait_past(dve, low_ready, grp.wait_free)
                    dst, ready = zfull[:, grp.wait_slot, :, :], full_ready
                else:
                    wait_past(dve, multiplied, grp.free)
                    dst, ready = z[:, grp.slot, :, :], z_ready
                dve.tensor_tensor(dst, xb[:, 2 * g:2 * g + 2, :], h[:, :].unsqueeze(1).broadcast_to([128, 2, N]),
                                  ALU.mult).then_inc(ready, 1)

            def low_part(grp):
                dve.wait_ge(high_ready, grp.kind_count)
                wait_past(dve, multiplied, grp.free)
                dve.tensor_tensor(zlow[:, grp.slot, :, :], zfull[:, grp.wait_slot, :, :],
                                  zhigh[:, grp.slot, :, :].bitcast(FP32), ALU.subtract).then_inc(low_ready, 1)

            def products(h, s, q, phase, last, between=None):
                waiting = []
                for g in range(XPAIRS):
                    if phase == "L1" and g % 2 == 0:
                        loads = 3 if g // 2 == QUADS - 1 else 2
                        dve.wait_ge(xb_in[g // 2], 16 * loads * (s + 1))
                    grp = Group(s, q, phase, g, last)
                    z12(h, g, grp)
                    if waiting and g >= waiting[0][0] + LOW_LAG:
                        low_part(waiting.pop(0)[1])
                    if grp.split:
                        waiting.append((g, grp))
                    if between:
                        between(g)
                for _, grp in waiting:
                    low_part(grp)
                dve.wait_ge(last_high, 2 * s + (1 if phase == "L1" else 2))
                grp = Group(s, q, phase, XPAIRS - 1, last)
                dve.tensor_tensor(zlast[H:128, :], z[H:128, grp.slot, 1, :], zlast[H:128, :].bitcast(FP32),
                                  ALU.subtract).then_inc(last_low, 1)
                if between:
                    between(XPAIRS)

            dve.wait_ge(const_in, 16 * N_CONST)
            dve.tensor_copy(wlast_high[:, :, :], wlast_sb[:, :, :]).then_inc(w_split, 1)
            dve.wait_ge(w_split, 1)
            dve.tensor_tensor(wlast_low[:, :, :], wlast_sb[0:H, :, :], wlast_high[0:H, :, :].bitcast(FP32),
                              ALU.subtract).then_inc(w_split, 1)
            for i in range(len(SPLIT)):
                dve.tensor_copy(whigh[:, i, :, :], w_stage[:, i, :, :]).then_inc(w_split, 1)
            for i in range(len(SPLIT)):
                dve.wait_ge(w_split, 2 + len(SPLIT))
                dve.tensor_tensor(wlow[:, i, :, :], w_stage[:, i, :, :], whigh[:, i, :, :].bitcast(FP32),
                                  ALU.subtract).then_inc(w_split, 1)
            products0(0)

            def step(bt, q, last):
                s = bt * CPB + q
                dve.wait_ge(h_ready[0], 2 * (s + 1))
                products(h1, s, q, "L1", last, between=lambda g: products0(s + 1) if g == Z0_AT and not last else None)
                dve.wait_ge(h_ready[1], 2 * (s + 1))
                products(h2, s, q, "L2", last)

            steps(dve, step)

            dve.wait_ge(dir_ready[2], NCHUNK)
            dve.wait_ge(sum2_done, ADDS * NBT - 1)
            dve.tensor_tensor(sum2[:, :], sum2[:, :], dir2[:, (CPB - 1) % 2, :], ALU.add).then_inc(last_folded, 1)
            dve.wait_ge(last_folded, 1)
            dve.wait_ge(folded, 4 * (NBT - 1))
            dve.tensor_tensor(half[:, 1, :], sum2[:, 0:N // 2], sum2[:, N // 2:N], ALU.add).then_inc(last_folded, 1)
            dve.wait_ge(last_folded, 2)
            dve.wait_ge(top_sum[0], NBT - 1)
            dve.tensor_tensor(feat[:, 1, :], half[:, 1, 0:BT], half[:, 1, BT:2 * BT], ALU.add).then_inc(last_folded, 1)

        @block.tensor
        def _(pe):
            pe.wait_ge(const_in, 16 * N_CONST)

            def select(c, bt, q):
                if q == 0:
                    pe.wait_ge(copied, SPT * (bt + 1))
                wait_past(pe, xdup_ready, c)
                wait_past(pe, z0_ready, G0 * c)
                for i in range(DQ):
                    ins = pe.transpose(dup[0:R0, i * BT:(i + 1) * BT],
                                       rows[:, q * DQ + i, :, :].rearrange("p k f -> p (k f)"), ident_sb[:, :])
                ins.then_inc(sel_ready, 1)

            def layer0(c, g, first=False):
                if g == 0 and not first:
                    pe.wait_ge(h_ready[0], 2 * c)
                    pe.wait_ge(dir_ready[0], c)
                pe.wait_ge(z0_ready, G0 * c + g + 1)
                for i, t in enumerate(layer0_tiles(g)):
                    rows = R0_LAST if t == T0 - 1 else R0
                    ins = pe.matmul(acc0[:, :], w0_sb[0:rows, t, :], z0[0:rows, t, :],
                                    start=(g == 0), stop=(g == G0 - 1 and i == len(layer0_tiles(g)) - 1))
                ins.then_inc(multiplied, 1)

            def layer12(acc, layer, s, g, grp):
                if grp.split:
                    k = SPLIT.index((layer, g))
                    pe.wait_ge(high_ready, grp.kind_count)
                    for i in range(2):
                        for part in (whigh, wlow):
                            pe.matmul(acc, part[:, k, i, :], zhigh[:, grp.slot, i, :], start=False, stop=False)
                    pe.wait_ge(low_ready, grp.kind_count)
                    for i in range(2):
                        ins = pe.matmul(acc, whigh[:, k, i, :], zlow[:, grp.slot, i, :], start=False, stop=False)
                else:
                    pe.wait_ge(z_ready, grp.kind_count)
                    for i in range(1 if g == XPAIRS - 1 else 2):
                        ins = pe.matmul(acc, w12_sb[:, WHOLE.index((layer, g)), i, :], z[:, grp.slot, i, :],
                                        start=(g == 0 and i == 0), stop=False)
                    if g == XPAIRS - 1:
                        pe.wait_ge(last_low, 2 * s + layer + 1)
                        pe.matmul(acc, wlast_low[:, layer, :], zlast[0:H, :], start=False, stop=False)
                        ins = pe.matmul(acc, wlast_high[:, layer, :], zlast[:, :], start=False, stop=True)
                ins.then_inc(multiplied, 1)

            def top_layer(i, bt):
                if i == 0:
                    wait_past(pe, top_ready[2], bt)
                    pe.wait_ge(folded, 4 * (bt + 1))
                    for m in range(M_TOP1 // 128):
                        ms = slice(m * 128, (m + 1) * 128)
                        pe.matmul(top[:, m, :], wt1_sb[:, 0, ms], feat[:, 0, :], start=True, stop=False)
                        pe.matmul(top[:, m, :], wt1_sb[:, 1, ms], feat[:, 1, :], start=False, stop=False)
                        ins = pe.matmul(top[:, m, :], wt1d_sb[:, ms], dense_sb[:, bass.ds(bt * BT, BT)], start=False, stop=True)
                elif i == 1:
                    pe.wait_ge(top_ready[0], bt + 1)
                    for m in range(M_TOP2 // 128):
                        for k in range(M_TOP1 // 128):
                            ins = pe.matmul(top[:, m, :], wt2_sb[:, k, m * 128:(m + 1) * 128], t1[:, k, :],
                                            start=(k == 0), stop=(k == M_TOP1 // 128 - 1))
                else:
                    pe.wait_ge(top_ready[1], bt + 1)
                    for k in range(M_TOP2 // 128):
                        ins = pe.matmul(top[0:1, 0, :], cols_sb[:, COL_W3 + k:COL_W3 + k + 1], t2[:, k, :],
                                        start=(k == 0), stop=(k == M_TOP2 // 128 - 1))
                ins.then_inc(top_sum[i], 1)

            def top_between(bt, q, phase, g):
                if not first_tile(bt) and (q, phase, g) in TOP_AT:
                    top_layer(TOP_AT.index((q, phase, g)), bt - 1)

            pe.wait_ge(early_copied, SPT)
            select(0, 0, 0)
            pe.wait_ge(w0_ready, 2)
            pe.wait_ge(w_split, 2 + 2 * len(SPLIT))
            for g in range(G0):
                layer0(0, g, first=True)
            select(1, 0, 1)

            def step(bt, q, last):
                s = bt * CPB + q
                wait_past(pe, h_ready[1], 2 * s)
                wait_past(pe, dir_ready[1], s)
                for g in range(XPAIRS):
                    layer12(acc1[:, :], 0, s, g, Group(s, q, "L1", g, last))
                    top_between(bt, q, "L1", g)
                if not last:
                    for g in range(G0):
                        layer0(s + 1, g)
                wait_past(pe, dir_ready[2], s)
                for g in range(XPAIRS):
                    layer12(acc2[:, :], 1, s, g, Group(s, q, "L2", g, last))
                    if g == SELECT_AT and two_more(bt, q):
                        select(s + 2, *((bt, q + 2) if q < CPB - 2 else (bt + 1, q + 2 - CPB)))
                    top_between(bt, q, "L2", g)

            steps(pe, step)

            pe.wait_ge(folded, 4 * NBT - 2)
            pe.wait_ge(top_ready[2], NBT - 1)
            pe.wait_ge(dir_ready[1], NCHUNK)
            for m in range(M_TOP1 // 128):
                if m == M_TOP1 // 128 - 1:
                    pe.wait_ge(dir_ready[2], NCHUNK)
                ms = slice(m * 128, (m + 1) * 128)
                pe.matmul(top_bank(0, m, True), wt1_sb[:, 0, ms], feat[:, 0, :], start=True, stop=False)
                pe.matmul(top_bank(0, m, True), wt1d_sb[:, ms], dense_sb[:, B - BT:B], start=False, stop=False)
            pe.wait_ge(last_folded, 3)
            for m in range(M_TOP1 // 128):
                pe.matmul(top_bank(0, m, True), wt1_sb[:, 1, m * 128:(m + 1) * 128], feat[:, 1, :],
                          start=False, stop=True).then_inc(top_sum[0], 1)
            for m in range(M_TOP2 // 128):
                for k in range(M_TOP1 // 128):
                    pe.wait_ge(top_ready[0], NBT + k)
                    ins = pe.matmul(top_bank(1, m, True), wt2_sb[:, k, m * 128:(m + 1) * 128], t1[:, k, :],
                                    start=(k == 0), stop=(k == M_TOP1 // 128 - 1))
                ins.then_inc(top_sum[1], 1)
            for k in range(M_TOP2 // 128):
                pe.wait_ge(top_ready[1], NBT + k)
                ins = pe.matmul(top[0:1, 0, :], cols_sb[:, COL_W3 + k:COL_W3 + k + 1], t2[:, k, :],
                                start=(k == 0), stop=(k == M_TOP2 // 128 - 1))
            ins.then_inc(top_sum[2], 1)


def column_vectors(inputs):
    b0, b1, b2, bt1, bt2, w3 = (np.asarray(inputs[n]).ravel() for n in
                                ("L0_rec_b0", "L0_rec_b1", "L0_rec_b2", "b_top1", "b_top2", "W_top3"))
    rows = [np.concatenate([b[i:i + H]] * 2) for b in (b0, b1) for i in (0, H)] + [b2]
    rows += list(bt1.reshape(-1, 128)) + list(bt2.reshape(-1, 128)) + list(w3.reshape(-1, 128))
    return np.ascontiguousarray(np.stack(rows).T)


def kernel(**inputs):
    import concourse.bacc as bacc
    from concourse.bass_utils import run_bass_kernel_spmd

    nc = bacc.Bacc("TRN2", target_bir_lowering=False, num_devices=1)
    w0 = np.asarray(inputs["L0_rec_W0"])
    f = np.arange(F)[None, :]
    g = (f + np.arange(SHIFTS)[:, None]) % F
    arrays = {"dense_t": np.ascontiguousarray(np.asarray(inputs["dense_ctx"]).T), "ids": np.asarray(inputs["ids"])}
    for i in range(F):
        arrays[f"tbl_{i}"] = np.asarray(inputs[f"tbl_{i}"])
    arrays.update(
        w0_fwd=np.ascontiguousarray(w0[(f * F + g).ravel()]), w0_rev=np.ascontiguousarray(w0[(g * F + f).ravel()]),
        w1=np.asarray(inputs["L0_rec_W1"]), w2=np.asarray(inputs["L0_rec_W2"]), wt1=np.asarray(inputs["W_top1"]),
        wt2=np.asarray(inputs["W_top2"]), columns=column_vectors(inputs),
        ident=np.eye(128, dtype=np.float32))
    aps = {name: nc.dram_tensor(f"in_{name}", a.shape, mybir.dt.from_np(a.dtype), kind="ExternalInput").ap()
           for name, a in arrays.items()}
    out = nc.dram_tensor("out_y", (1, B), FP32, kind="ExternalOutput").ap()
    x_dram = nc.dram_tensor("x_dram", (2, 2 * F, N), FP32, kind="Internal").ap()
    tables = [aps.pop(f"tbl_{i}") for i in range(F)]
    build(nc, tables=tables, x_dram=x_dram, out=out, **aps)
    r = run_bass_kernel_spmd(nc, [{f"in_{name}": a for name, a in arrays.items()}], core_ids=[0])
    return np.asarray(r.results[0]["out_y"]).reshape(B, 1)
```
